# Optimizing a Trainium2 kernel written in Bass

```python
import numpy as np
import jax
import jax.numpy as jnp

def _softmax(x, axis=-1):
    return jax.nn.softmax(x, axis=axis)

def _gelu(x):
    return jax.nn.gelu(x, approximate=True)

def _silu(x):
    return jax.nn.silu(x)

def _sigmoid(x):
    return jax.nn.sigmoid(x)

def _layernorm(x, axis=-1, eps=1e-05):
    m = jnp.mean(x, axis=axis, keepdims=True)
    v = jnp.var(x, axis=axis, keepdims=True)
    return (x - m) / jnp.sqrt(v + eps)

def _scatter_add(tgt, idx, src, axis=0):
    return tgt.at[idx].add(src)

def _segment_sum(src, seg, n):
    return jax.ops.segment_sum(src, seg, n)
kernel_name = 'mk_macaron_d1_jaxref_r8_2eb955'

def setup_inputs(seed: int=0):
    np.random.seed(seed)
    _w = jnp.asarray

    def _L0_attn_setup():
        import jax, jax.numpy as jnp
        import numpy as np
        import math
        B, T, C = (2, 256, 128)
        H, L = (16, 64)
        DH = C // H
        DHE = DH // 2
        THETA = 10000.0

        def _rope_cache(t, dim):
            inv_freq = 1.0 / THETA ** (jnp.arange(0, dim, 2, dtype=jnp.float32) / dim)
            freqs = jnp.arange(t, dtype=jnp.float32)[:, None] * inv_freq[None, :]
            emb = jnp.concatenate((freqs, freqs), axis=-1)
            return (jnp.cos(emb), jnp.sin(emb))

        def _apply_rope(x, cos, sin):
            x1 = x[..., 0::2]
            x2 = x[..., 1::2]
            rot = jnp.stack((-x2, x1), axis=-1).reshape(x.shape)
            return x * cos[None, None] + rot * sin[None, None]
        key = jax.random.key(seed)
        ks = jax.random.split(key, 10)
        s = 0.02
        return {'x': jax.random.normal(ks[0], (B, T, C), jnp.float32), 'Wq_down': jax.random.normal(ks[1], (C, H * L), jnp.float32) * s, 'Wk_down': jax.random.normal(ks[2], (C, H * L), jnp.float32) * s, 'Wv_down': jax.random.normal(ks[3], (C, H * L), jnp.float32) * s, 'Wq_up_c': jax.random.normal(ks[4], (L, DHE), jnp.float32) * s, 'Wq_up_e': jax.random.normal(ks[5], (L, DHE), jnp.float32) * s, 'Wk_up_c': jax.random.normal(ks[6], (L, DHE), jnp.float32) * s, 'Wk_up_e': jax.random.normal(ks[7], (L, DHE), jnp.float32) * s, 'Wv_up': jax.random.normal(ks[8], (L, DH), jnp.float32) * s, 'Wc': jax.random.normal(ks[9], (C, C), jnp.float32) * s}
    _L0_attn_in = _L0_attn_setup()

    def _L0_ffn_setup():
        import jax, jax.numpy as jnp
        import numpy as np
        TOP_K = 2
        key = jax.random.key(seed)
        k1, k2, k3 = jax.random.split(key, 3)
        B, S, D, E = (8, 256, 128, 8)
        x = jax.random.normal(k1, (B, S, D), dtype=jnp.float32)
        gate_w = jax.random.normal(k2, (E, D), dtype=jnp.float32) * (1.0 / np.sqrt(D))
        gate_b = jnp.zeros((E,), dtype=jnp.float32)
        expert_w = jax.random.normal(k3, (E, D, D), dtype=jnp.float32) * (1.0 / np.sqrt(D))
        expert_b = jnp.zeros((E, D), dtype=jnp.float32)
        return {'x': x, 'gate_w': gate_w, 'gate_b': gate_b, 'expert_w': expert_w, 'expert_b': expert_b}
    _L0_ffn_in = _L0_ffn_setup()
    _d = {'L0_attn_x': _L0_attn_in['x'], 'L0_attn_Wq_down': _L0_attn_in['Wq_down'], 'L0_attn_Wk_down': _L0_attn_in['Wk_down'], 'L0_attn_Wv_down': _L0_attn_in['Wv_down'], 'L0_attn_Wq_up_c': _L0_attn_in['Wq_up_c'], 'L0_attn_Wq_up_e': _L0_attn_in['Wq_up_e'], 'L0_attn_Wk_up_c': _L0_attn_in['Wk_up_c'], 'L0_attn_Wk_up_e': _L0_attn_in['Wk_up_e'], 'L0_attn_Wv_up': _L0_attn_in['Wv_up'], 'L0_attn_Wc': _L0_attn_in['Wc'], 'L0_ffn_gate_w': _L0_ffn_in['gate_w'], 'L0_ffn_gate_b': _L0_ffn_in['gate_b'], 'L0_ffn_expert_w': _L0_ffn_in['expert_w'], 'L0_ffn_expert_b': _L0_ffn_in['expert_b']}
    _x0 = _d['L0_attn_x']
    _d['L0_attn_x'] = jax.random.normal(jax.random.fold_in(jax.random.key(seed), 1), (4, 1024, 128), dtype=_x0.dtype)
    del _x0
    return _d

def reference(L0_attn_x, L0_attn_Wq_down, L0_attn_Wk_down, L0_attn_Wv_down, L0_attn_Wq_up_c, L0_attn_Wq_up_e, L0_attn_Wk_up_c, L0_attn_Wk_up_e, L0_attn_Wv_up, L0_attn_Wc, L0_ffn_gate_w, L0_ffn_gate_b, L0_ffn_expert_w, L0_ffn_expert_b):

    def _L0_attn_ref(x, Wq_down, Wk_down, Wv_down, Wq_up_c, Wq_up_e, Wk_up_c, Wk_up_e, Wv_up, Wc):
        import jax, jax.numpy as jnp
        import numpy as np
        import math
        B, T, C = (2, 256, 128)
        H, L = (16, 64)
        DH = C // H
        DHE = DH // 2
        THETA = 10000.0

        def _rope_cache(t, dim):
            inv_freq = 1.0 / THETA ** (jnp.arange(0, dim, 2, dtype=jnp.float32) / dim)
            freqs = jnp.arange(t, dtype=jnp.float32)[:, None] * inv_freq[None, :]
            emb = jnp.concatenate((freqs, freqs), axis=-1)
            return (jnp.cos(emb), jnp.sin(emb))

        def _apply_rope(x, cos, sin):
            x1 = x[..., 0::2]
            x2 = x[..., 1::2]
            rot = jnp.stack((-x2, x1), axis=-1).reshape(x.shape)
            return x * cos[None, None] + rot * sin[None, None]
        b, t, c = x.shape
        q_lat = (x @ Wq_down).reshape(b, t, H, L)
        k_lat = (x @ Wk_down).reshape(b, t, H, L)
        v_lat = (x @ Wv_down).reshape(b, t, H, L)
        q_c = jnp.einsum('bthl,ld->bhtd', q_lat, Wq_up_c)
        q_e = jnp.einsum('bthl,ld->bhtd', q_lat, Wq_up_e)
        k_c = jnp.einsum('bthl,ld->bhtd', k_lat, Wk_up_c)
        k_e = jnp.einsum('bthl,ld->bhtd', k_lat, Wk_up_e)
        v = jnp.einsum('bthl,ld->bhtd', v_lat, Wv_up)
        cos, sin = _rope_cache(t, DHE)
        q = jnp.concatenate([q_c, _apply_rope(q_e, cos, sin)], axis=-1)
        k = jnp.concatenate([k_c, _apply_rope(k_e, cos, sin)], axis=-1)
        scale = 1.0 / math.sqrt(DH)
        scores = jnp.einsum('bhqd,bhkd->bhqk', q, k) * scale
        causal = jnp.tril(jnp.ones((t, t), dtype=bool))
        scores = jnp.where(causal[None, None], scores, -jnp.inf)
        att = jax.nn.softmax(scores, axis=-1)
        y = jnp.einsum('bhqk,bhkd->bhqd', att, v)
        y = y.transpose(0, 2, 1, 3).reshape(b, t, c)
        return y @ Wc

    def _L0_ffn_ref(x, gate_w, gate_b, expert_w, expert_b):
        import jax, jax.numpy as jnp
        import numpy as np
        TOP_K = 2
        gate = jnp.einsum('bsd,ed->bse', x, gate_w) + gate_b
        _, idx = jax.lax.top_k(gate, TOP_K)
        E = gate_w.shape[0]
        flat_idx = idx.reshape(-1)
        counts = jnp.zeros((E,), dtype=x.dtype).at[flat_idx].add(1.0)
        expert_out = jax.nn.relu(jnp.einsum('bsd,ehd->bseh', x, expert_w) + expert_b)
        total = flat_idx.size
        out = jnp.einsum('bseh,e->bsh', expert_out, counts) / total
        return out
    x = L0_attn_x
    x = x + 0.5 * _L0_ffn_ref(_layernorm(x, axis=-1), L0_ffn_gate_w, L0_ffn_gate_b, L0_ffn_expert_w, L0_ffn_expert_b)
    x = x + _L0_attn_ref(_layernorm(x, axis=-1), L0_attn_Wq_down, L0_attn_Wk_down, L0_attn_Wv_down, L0_attn_Wq_up_c, L0_attn_Wq_up_e, L0_attn_Wk_up_c, L0_attn_Wk_up_e, L0_attn_Wv_up, L0_attn_Wc)
    x = x + 0.5 * _L0_ffn_ref(_layernorm(x, axis=-1), L0_ffn_gate_w, L0_ffn_gate_b, L0_ffn_expert_w, L0_ffn_expert_b)
    return x

_drawn_inputs = setup_inputs


def setup_inputs(seed=0):
    import zlib

    import numpy as np

    out = dict(_drawn_inputs(seed))
    spreads = {'L0_ffn_gate_b': (0.0, 0.345), 'L0_ffn_expert_b': (0.0, 0.351)}
    factors = {'L0_attn_Wq_down': 8.0,
     'L0_attn_Wk_down': 8.0,
     'L0_attn_Wv_down': 8.0,
     'L0_attn_Wq_up_c': 8.0,
     'L0_attn_Wq_up_e': 8.0,
     'L0_attn_Wk_up_c': 8.0,
     'L0_attn_Wk_up_e': 8.0,
     'L0_attn_Wv_up': 8.0,
     'L0_attn_Wc': 8.0,
     'L0_ffn_gate_w': 3.207}
    for name, (base, spread) in spreads.items():
        noise = np.random.default_rng([zlib.crc32(name.encode()), seed]).standard_normal(out[name].shape)
        drawn = base * np.exp(spread * noise) if base else spread * noise
        out[name] = jnp.asarray(drawn.astype(out[name].dtype))
    for name, factor in factors.items():
        out[name] = (out[name] * factor).astype(out[name].dtype)
    return out
```

```python
from contextlib import ExitStack

import concourse.bass as bass
import numpy as np
from concourse import mybir

F32 = mybir.dt.float32
BF16 = mybir.dt.bfloat16
ALU = mybir.AluOpType
ACT = mybir.ActivationFunctionType
AX = mybir.AxisListType
ds = bass.ds

P = 128
B, T, C = 4, 1024, 128
H, L, DH = 16, 64, 8
DHE = DH // 2
E = 8
TOP_K = 2
N_TOK = B * T
N_TILE = N_TOK // P
CH = 512
TPC = CH // P
PAIRS = N_TOK // (2 * CH)
EPS = 1e-5
BIG = 3.0e38

HG = 4
G = H // HG
N_GROUP = B * G
KT = T // P
SCALE = 1.0 / float(np.sqrt(DH))
HROW = 32
PRODUCTS = [(0, 0), (0, 1), (0, 2), (1, 0), (1, 1), (2, 0)]
M_ROW = 96
K_ALL = M_ROW + 2

BATCHES = [[[(j, 0, 0)] for j in range(HG)]]
BATCHES += [[[(j, a, 0), (j, KT - a, T - P * a)] for j in range(HG)] for a in range(1, KT // 2)]
BATCHES += [[[(j, 4, 0), (j + 1, 4, CH)] for j in range(0, HG, 2)]]
SLOTS = [slot for batch in BATCHES for slot in batch]
BATCH_OF = [b for b, batch in enumerate(BATCHES) for _ in batch]
N_SLOT = len(SLOTS)
N_PBUF = N_SLOT // 2
N_BATCH = len(BATCHES)
LAST_SLOT = [max(s for s in range(N_SLOT) if BATCH_OF[s] == b) for b in range(N_BATCH)]


def value_steps(b):
    per_head = {j: [] for j in range(HG)}
    for s in range(N_SLOT):
        if BATCH_OF[s] != b:
            continue
        for j, kt, off in SLOTS[s]:
            q = kt * P
            while q < T:
                w = min(CH - q % CH, T - q)
                per_head[j].append((j, kt, s, off + q - kt * P, q, w))
                q += w
    return [[per_head[j][i] for j in range(HG)] for i in range(len(per_head[0]))]


MAX_UNITS = []
for _j in range(HG):
    MAX_UNITS += [(_j, [(qt, qt, 1) for qt in range(4)]), (_j, [(qt, qt, 1) for qt in range(4, 8)])]
    MAX_UNITS += [(_j, u) for u in (
        [(7, 0, 4)], [(7, 4, 3), (1, 0, 1)], [(6, 0, 4)], [(6, 4, 2), (2, 0, 2)],
        [(5, 0, 4)], [(5, 4, 1), (3, 0, 3)], [(4, 0, 4)])]
    if _j % 2:
        MAX_UNITS.append((_j // 2, None))
N_UNIT = len(MAX_UNITS)


def atleast(eng, sem, value):
    if isinstance(value, int) and value <= 0:
        return
    eng.wait_ge(sem, value)


def reached(eng, sem, count):
    eng.wait_ge(sem, count + 1)


def apart(eng, passed):
    eng.sem_inc(passed, 1)


def build(nc, x, wq_t, wk_t, wv_t, q_c, q_e, k_c, k_e, v_up, wc, gate_wt, gate_b, exp_wt, exp_bt,
          cos, sin, out):
    ctx = ExitStack()
    with ctx:
        def sb(name, shape, dt=F32):
            return ctx.enter_context(nc.sbuf_tensor(name, shape, dt))

        def sem(name):
            return ctx.enter_context(nc.semaphore(name))

        def sem2(name):
            return [sem(f"{name}{p}") for p in range(2)]

        bank = [ctx.enter_context(nc.psum_tensor(f"bank{i}", [P, CH], F32)) for i in range(2)]
        work = [ctx.enter_context(nc.psum_tensor(f"work{i}", [P, CH], F32)) for i in range(2)]
        st_ps = [ctx.enter_context(nc.psum_tensor(f"st{i}", [P, 2 * CH], F32)) for i in range(2)]
        y_ps = [bank[0], bank[1]]
        qk_ps = [st_ps[0][:, 0:CH], st_ps[0][:, CH:2 * CH], st_ps[1][:, 0:CH], st_ps[1][:, CH:2 * CH]]
        exp_ps = [bank[0], bank[1], st_ps[0][:, 0:CH], st_ps[1][:, 0:CH]]

        x_sb = sb("x_sb", [P, N_TILE, C])
        xnt_all = sb("xnt_all", [P, N_TOK])
        ident = sb("ident", [P, P])
        causal = sb("causal", [P, P])
        ones = sb("ones", [P, P])
        neg_half = sb("neg_half", [P, TPC])
        rank = sb("rank", [P, E])
        gw = sb("gw", [P, E])
        gb = sb("gb", [P, E])
        ew = sb("ew", [P, E, C])
        eb = sb("eb", [P, E])
        ews = sb("ews", [P, E, C])
        weight = sb("weight", [P, E])
        neg_b = sb("neg_b", [P, E])
        b_sum = sb("b_sum", [P, 1])
        up = {n: sb(f"up_{n}", [P, 2, 2, DH]) for n in "qkv"}
        w_qk = {n: sb(f"w_{n}", [P, 2, G, DH, HG]) for n in "qk"}
        w_v = sb("w_v", [P, C])
        wc_sb = sb("wc_sb", [P, C])
        cos_sb = sb("cos_sb", [P, T])
        sin_sb = sb("sin_sb", [P, T])
        stats = [sb(f"stats{p}", [P, TPC, 6]) for p in range(2)]
        moments = [sb(f"moments{p}", [P, TPC, 2]) for p in range(2)]
        var_eps = [sb(f"var_eps{p}", [P, TPC]) for p in range(2)]
        rstd = [sb(f"rstd{p}", [P, TPC]) for p in range(2)]
        xn = [sb(f"xn{p}", [P, TPC, C]) for p in range(2)]
        xnt = [sb(f"xnt{p}", [P, CH]) for p in range(2)]
        acc = [sb(f"acc{p}", [P, CH]) for p in range(2)]
        gates = sb("gates", [P, N_TILE, E])
        gate_tmp = sb("gate_tmp", [P, N_TILE, E])
        first = sb("first", [P, N_TILE, E])
        second = sb("second", [P, N_TILE, E])
        best = sb("best", [P, N_TILE, 1])
        counts = sb("counts", [P, E])
        parts = [sb(f"parts{p}", [P, 2, 3, CH], BF16) for p in range(2)]
        v_all = sb("v_all", [P, B * G, KT, HG * DH])
        stack_q = [sb(f"stack_q{p}", [P, HG, T], BF16) for p in range(2)]
        stack_k = [sb(f"stack_k{p}", [P, HG, T], BF16) for p in range(2)]
        v_st = [sb(f"v_st{p}", [P, KT, HG, HROW]) for p in range(2)]
        prob = [sb(f"prob{i}", [P, T]) for i in range(N_PBUF)]
        down = {n: prob[i][:].rearrange("p (m c) -> p m c", c=C) for i, n in enumerate("qkv")}
        rot_a, rot_b, rest = (prob[i][:].rearrange("p (s t) -> p s t", s=2) for i in (3, 4, 5))
        pmax = sb("pmax", [P, HG, KT, 3])
        neg_max = sb("neg_max", [P, HG * KT])
        junk = sb("junk", [P, 2, 4, P])
        m_parts = [sb(f"m_parts{h}", [2 * KT, 2, P], BF16) for h in range(2)]
        y_sb = [sb(f"y_sb{p}", [P, T]) for p in range(2)]
        y_t = [y_sb[p][:, 0:CH] for p in range(2)]
        den_t = [y_sb[p][:, CH:T] for p in range(2)]

        parts_dram = nc.dram_tensor("parts_dram", [2, 3, B, P, T], BF16, kind="Internal").ap()
        y_dram = nc.dram_tensor("y_dram", [2, N_GROUP, HG, DH, T], F32, kind="Internal").ap()
        parts_by_group = parts_dram.rearrange("s c b (g f) t -> s c (b g) f t", g=G)

        x_loaded = sem("x_loaded")
        w_loaded = sem("w_loaded")
        pool_zeroed = sem("pool_zeroed")
        consts = sem("consts")
        dve_passed, pool_passed, sp_passed = sem("dve_passed"), sem("pool_passed"), sem("sp_passed")
        rot_w = sem("rot_w")
        w_prod = sem("w_prod")
        w_ready = sem("w_ready")
        dve = sem("dve")
        xn_stat = {f: sem2(f"xn_stat_{f}") for f in range(3)}
        xn_aggr = {f: sem2(f"xn_aggr_{f}") for f in range(3)}
        var_ready = {f: sem2(f"var_ready_{f}") for f in range(3)}
        rstd_ready = {f: sem2(f"rstd_ready_{f}") for f in range(3)}
        xn_ready = {f: sem2(f"xn_ready_{f}") for f in range(3)}
        tp_ready = {f: sem2(f"tp_ready_{f}") for f in range(3)}
        xnt_ready = {f: sem2(f"xnt_ready_{f}") for f in range(3)}
        xnt_saved = {f: sem2(f"xnt_saved_{f}") for f in (0, 2)}
        gate_ready = {f: sem2(f"gate_ready_{f}") for f in (0, 2)}
        gate_used = {f: sem2(f"gate_used_{f}") for f in (0, 2)}
        cnt_ready = {f: sem(f"cnt_ready_{f}") for f in (0, 2)}
        cnt_sum = {f: sem(f"cnt_sum_{f}") for f in (0, 2)}
        ews_ready = {f: sem(f"ews_ready_{f}") for f in (0, 2)}
        exp_ready = {f: [sem(f"exp_ready_{f}_{i}") for i in range(4)] for f in (0, 2)}
        exp_used = {f: [sem(f"exp_used_{f}_{i}") for i in range(4)] for f in (0, 2)}
        back_ready = {f: sem2(f"back_ready_{f}") for f in (0, 2)}
        x_done = {f: sem2(f"x_done_{f}") for f in (0, 2)}
        out_written = sem("out_written")

        qk_ready = [sem(f"qk_ready{i}") for i in range(4)]
        qk_used = [sem(f"qk_used{i}") for i in range(4)]
        v_ready = sem2("v_ready")
        v_used = sem("v_used")
        rotated = sem("rotated")
        rot_sum = sem("rot_sum")
        hi_ready = sem("hi_ready")
        rest_ready = sem("rest_ready")
        mid_ready = sem("mid_ready")
        lo_ready = sem("lo_ready")
        parts_written = sem2("parts_written")

        stack_init = sem("stack_init")
        stack_loaded = sem2("stack_loaded")
        v_st_ready = sem("v_st_ready")
        st_ready = sem("st_ready")
        exp_done = sem("exp_done")
        masked = sem("masked")
        pv_done = sem("pv_done")
        y_copied = sem("y_copied")
        y_written = sem2("y_written")
        unit_ready = [sem(f"unit_ready{i}") for i in range(2)]
        unit_used = [sem(f"unit_used{i}") for i in range(2)]
        neg_max_ready = sem("neg_max_ready")
        m_hi = sem("m_hi")
        m_loaded = sem("m_loaded")

        y_loaded = sem2("y_loaded")
        y_recip = sem2("y_recip")
        y_norm = sem2("y_norm")
        attn_ready = sem2("attn_ready")
        attn_added = sem2("attn_added")

        start_at_one = [lo_ready, rotated, v_used]
        for pair in (v_ready, parts_written, y_written, attn_ready, attn_added):
            start_at_one += pair
        for by_front in (tp_ready, xnt_ready, gate_ready, xnt_saved, gate_used, exp_used, back_ready, x_done):
            for several in by_front.values():
                start_at_one += several

        block = ctx.enter_context(nc.Block())

        @block.sync
        def _(sp):
            for b in range(B):
                sp.dma_start(x_sb[:, b * KT:(b + 1) * KT, :],
                             x[b * T:(b + 1) * T, :].rearrange("(t p) c -> p t c", p=P)).then_inc(x_loaded, 16)
            sp.dma_start(gw[:], gate_wt).then_inc(w_loaded, 16)
            sp.dma_start(gb[:], gate_b.rearrange("(a e) -> a e", a=1).broadcast_to([P, E])).then_inc(w_loaded, 16)
            sp.dma_start(ew[:], exp_wt).then_inc(w_loaded, 16)
            sp.dma_start(eb[:], exp_bt).then_inc(w_loaded, 16)
            for n, src in (("q", wq_t), ("k", wk_t), ("v", wv_t)):
                sp.dma_start(down[n], src).then_inc(w_loaded, 16)
            sp.dma_start(wc_sb[:], wc).then_inc(w_loaded, 16)
            sp.dma_start(cos_sb[:], cos).then_inc(w_loaded, 16)
            sp.dma_start(sin_sb[:], sin).then_inc(w_loaded, 16)
            sp.wait_ge(pool_zeroed, 3)
            for i in range(2):
                rows = slice(i * L, (i + 1) * L)
                sp.dma_start(up["v"][rows, 0, i, :], v_up).then_inc(w_loaded, 16)
                for n, c_part, e_part in (("q", q_c, q_e), ("k", k_c, k_e)):
                    sp.dma_start(up[n][rows, 0, i, 0:DHE], c_part).then_inc(w_loaded, 16)
                    sp.dma_start(up[n][rows, 0, i, DHE:DH], e_part).then_inc(w_loaded, 16)

            with sp.Fori(0, PAIRS) as it:
                for p in range(2):
                    reached(sp, lo_ready, 2 * (2 * it + p) + 2)
                    for s in range(2):
                        sp.dma_start(
                            parts_dram[s, :, ds(it, 1), :, p * CH:(p + 1) * CH].rearrange("c a f t -> (a f) c t"),
                            parts[p][:, s, :, :]).then_inc(parts_written[p], 16)

            def load_stacks(n, p):
                for side, stack in ((0, stack_q[p]), (1, stack_k[p])):
                    i = 0
                    for row, (a, b) in enumerate(PRODUCTS):
                        part = (a, b)[side]
                        sp.dma_start(stack[row * DH:(row + 1) * DH, :, :],
                                     parts_by_group[side, part, ds(n, 1), :, :].rearrange(
                                         "a (d j) t -> (a d) j t", j=HG)).then_inc(stack_loaded[p], 16)

            def load_maxima(n, p):
                for h in range(2):
                    u = MAX_UNITS.index((h, None))
                    sp.wait_ge(unit_used[u % 2], (N_UNIT // 2) * n + u // 2 + 1)
                    for c in range(2):
                        sp.dma_start(stack_q[p][M_ROW + c:M_ROW + c + 1, 2 * h:2 * h + 2, :].rearrange(
                                         "a j (k t) -> a (j k) t", t=P),
                                     m_parts[h][:, c, :]).then_inc(m_loaded, 16)

            def store_y(n, p):
                sp.wait_ge(y_copied, 2 * n + 2)
                apart(sp, sp_passed)
                for j in range(HG):
                    for c in range(2):
                        row = j * HROW + c * DH
                        sp.dma_start(y_dram[c, ds(n, 1), j, :, :].rearrange("a r t -> (a r) t"),
                                     y_sb[p][row:row + DH, :]).then_inc(y_written[p], 16)

            def group(n, p, last=False):
                if not last:
                    atleast(sp, st_ready, N_SLOT * n)
                    load_stacks(n + 1, 1 - p)
                    load_maxima(n + 1, 1 - p)
                store_y(n, p)

            for p in range(2):
                reached(sp, parts_written[p], 32 * PAIRS)
            sp.wait_ge(stack_init, 10)
            load_stacks(0, 0)
            load_maxima(0, 0)
            group(0, 0)
            with sp.Fori(0, N_GROUP // 2 - 1) as it:
                group(2 * it + 1, 1)
                group(2 * it + 2, 0)
            group(N_GROUP - 1, 1, last=True)

            for p in range(2):
                reached(sp, y_written[p], 16 * 2 * HG * (N_GROUP // 2))
            y_rows = y_dram.rearrange("c (b g) j r t -> c b (g j r) t", b=B)
            with sp.Fori(0, PAIRS) as it:
                for p in range(2):
                    reached(sp, attn_ready[p], it)
                    for c, tile in enumerate((y_t[p], den_t[p])):
                        sp.dma_start(tile, y_rows[c, ds(it, 1), :, p * CH:(p + 1) * CH].rearrange(
                            "a r t -> (a r) t")).then_inc(y_loaded[p], 16)

            with sp.Fori(0, PAIRS) as it:
                for p in range(2):
                    reached(sp, x_done[2][p], it + 1)
                    sp.dma_start(out[ds(it * 2 * CH + p * CH, CH), :].rearrange("(t p) c -> p t c", p=P),
                                 x_sb[:, ds(it * 2 * TPC + p * TPC, TPC), :]).then_inc(out_written, 16)
            sp.wait_ge(out_written, 16 * 2 * PAIRS)

        @block.gpsimd
        def _(pool):
            for n in "qkv":
                nc.gpsimd.memset(up[n][:], 0.0).then_inc(pool_zeroed, 1)
            nc.gpsimd.memset(ones[:], 1.0).then_inc(pool_zeroed, 1)
            nc.gpsimd.memset(junk[:, 0, 0, :], 0.0).then_inc(pool_zeroed, 1)
            nc.gpsimd.memset(neg_half[:], -0.5).then_inc(consts, 1)
            for e in range(E):
                nc.gpsimd.memset(rank[:, e:e + 1], float(E - e)).then_inc(consts, 1)
            pool.wait_ge(pool_zeroed, 5)
            nc.gpsimd.affine_select(out=ident[:], in_=ones[:], compare_op=ALU.is_equal, fill=0.0, base=0,
                                    pattern=[[-1, P]], channel_multiplier=1).then_inc(consts, 1)
            nc.gpsimd.affine_select(out=causal[:], in_=junk[:, 0, 0, :], compare_op=ALU.is_ge, fill=-BIG, base=0,
                                    pattern=[[-1, P]], channel_multiplier=1).then_inc(consts, 1)
            for p in range(2):
                for tile in (stack_q[p], stack_k[p], v_st[p]):
                    nc.gpsimd.memset(tile[:], 0.0).then_inc(stack_init, 1)
            pool.wait_ge(stack_init, 6)
            for p in range(2):
                nc.gpsimd.memset(v_st[p][:, :, :, DH:2 * DH], 1.0).then_inc(stack_init, 1)
            pool.wait_ge(stack_init, 8)
            for p in range(2):
                nc.gpsimd.memset(stack_k[p][M_ROW:P, :, :], 1.0).then_inc(stack_init, 1)
            pool.wait_ge(stack_init, 10)

            def inverse_deviations(f, it, p):
                pool.wait_ge(var_ready[f][p], it + 1)
                nc.gpsimd.tensor_tensor(rstd[p][:], var_eps[p][:], neg_half[:], ALU.pow).then_inc(rstd_ready[f][p], 1)

            def save_transposed(f, it, p):
                reached(pool, xnt_ready[f][p], it + 1)
                nc.gpsimd.tensor_copy(xnt_all[:, ds(it * 2 * CH + p * CH, CH)], xnt[p][:]).then_inc(xnt_saved[f][p], 1)

            def ffn_front(f):
                with pool.Fori(0, PAIRS) as it:
                    for p in range(2):
                        inverse_deviations(f, it, p)
                    for p in range(2):
                        save_transposed(f, it, p)

            pool.wait_ge(consts, 11)
            ffn_front(0)

            with pool.Fori(0, PAIRS) as it:
                for p in range(2):
                    inverse_deviations(1, it, p)
                for p in range(2):
                    n = 2 * it + p
                    for s in range(2):
                        reached(pool, rotated, 4 * n + 2 * s + 2)
                        nc.gpsimd.tensor_tensor(rot_a[:, s, :], rot_a[:, s, :], rot_b[:, s, :],
                                                ALU.add).then_inc(rot_sum, 1)
                    for s in range(2):
                        pool.wait_ge(hi_ready, 2 * n + s + 1)
                        nc.gpsimd.tensor_tensor(rest[:, s, :], rot_a[:, s, :], parts[p][:, s, 0, :],
                                                ALU.subtract).then_inc(rest_ready, 1)
                    for s in range(2):
                        pool.wait_ge(mid_ready, 2 * n + s + 1)
                        nc.gpsimd.tensor_tensor(parts[p][:, s, 2, :], rest[:, s, :], parts[p][:, s, 1, :],
                                                ALU.subtract).then_inc(lo_ready, 1)

            def stage_values(n, p):
                atleast(pool, pv_done, N_BATCH * (n - 1))
                nc.gpsimd.tensor_copy(v_st[p][:, :, :, 0:DH], v_all[:, ds(n, 1), :, :].rearrange(
                    "p a k (j d) -> p (a k) j d", d=DH)).then_inc(v_st_ready, 1)

            def group(n, p, last=False):
                for s in range(N_SLOT):
                    atleast(pool, exp_done, N_SLOT * n + s + 1)
                    apart(pool, pool_passed)
                    for i, (j, kt, off) in enumerate(SLOTS[s]):
                        tile = prob[s % N_PBUF][:, off:off + P]
                        ins = nc.gpsimd.affine_select(out=tile, in_=tile, compare_op=ALU.is_ge, fill=0.0, base=0,
                                                      pattern=[[1, P]], channel_multiplier=-1)
                    ins.then_inc(masked, 1)
                    if s == 9 and not last:
                        stage_values(n + 1, 1 - p)

            pool.wait_ge(stack_init, 10)
            reached(pool, v_used, 2 * PAIRS)
            stage_values(0, 0)
            group(0, 0)
            with pool.Fori(0, N_GROUP // 2 - 1) as it:
                group(2 * it + 1, 1)
                group(2 * it + 2, 0)
            group(N_GROUP - 1, 1, last=True)

            with pool.Fori(0, PAIRS) as it:
                for p in range(2):
                    pool.wait_ge(y_recip[p], it + 1)
                    nc.gpsimd.tensor_tensor(y_t[p], y_t[p], den_t[p], ALU.mult).then_inc(y_norm[p], 1)
                for p in range(2):
                    inverse_deviations(2, it, p)
                for p in range(2):
                    save_transposed(2, it, p)

        @block.scalar
        def _(act):
            for one in start_at_one:
                act.sem_inc(one, 1)

            def copy_transposed(f, it, p):
                reached(act, tp_ready[f][p], it + 1)
                if f == 1:
                    reached(act, v_ready[p], it)
                else:
                    reached(act, gate_ready[f][p], it)
                    reached(act, xnt_saved[f][p], it)
                nc.scalar.copy(xnt[p][:], work[p][:]).then_inc(xnt_ready[f][p], 1)

            def front(f):
                with act.Fori(0, PAIRS) as it:
                    for p in range(2):
                        copy_transposed(f, it, p)

            front(0)

            with act.Fori(0, PAIRS) as it:
                for p in range(2):
                    copy_transposed(1, it, p)
                for p in range(2):
                    n = 2 * it + p
                    for s in range(2):
                        act.wait_ge(rot_sum, 2 * n + s + 1)
                        reached(act, parts_written[p], 32 * it)
                        nc.scalar.copy(parts[p][:, s, 0, :], rot_a[:, s, :]).then_inc(hi_ready, 1)
                    reached(act, v_ready[p], it + 1)
                    nc.scalar.copy(v_all[:, ds(it * G, G), p * TPC:(p + 1) * TPC, :],
                                   bank[0][:].rearrange("p (k g f) -> p g k f", k=TPC, g=G)).then_inc(v_used, 1)
                    for s in range(2):
                        act.wait_ge(rest_ready, 2 * n + s + 1)
                        nc.scalar.copy(parts[p][:, s, 1, :], rest[:, s, :]).then_inc(mid_ready, 1)

            def group(n, p, last=False):
                for s in range(N_SLOT):
                    act.wait_ge(st_ready, N_SLOT * n + s + 1)
                    if s >= N_PBUF:
                        atleast(act, pv_done, N_BATCH * n + BATCH_OF[s - N_PBUF] + 1)
                    else:
                        atleast(act, pv_done, N_BATCH * (n - 1) + BATCH_OF[s + N_PBUF] + 1)
                    nc.scalar.activation(prob[s % N_PBUF][:], st_ps[s % 2][:], ACT.Exp,
                                         scale=SCALE).then_inc(exp_done, 1)

            group(0, 0)
            with act.Fori(0, N_GROUP // 2 - 1) as it:
                group(2 * it + 1, 1)
                group(2 * it + 2, 0)
            group(N_GROUP - 1, 1, last=True)

            front(2)

        @block.vector
        def _(v):
            chain = [0]

            def link(ins):
                chain[0] += 1
                ins.then_inc(dve, 1)
                v.wait_ge(dve, chain[0])

            def statistics(f, it, p):
                tile = it * 2 * TPC + p * TPC
                for t in range(TPC):
                    ins = nc.vector.bn_stats(stats[p][:, t, :], x_sb[:, ds(tile + t, 1), :].rearrange("p a c -> p (a c)"))
                ins.then_inc(xn_stat[f][p], 1)
                v.wait_ge(xn_stat[f][p], it + 1)
                apart(v, dve_passed)
                for t in range(TPC):
                    ins = nc.vector.bn_aggr(moments[p][:, t, :], stats[p][:, t, :])
                ins.then_inc(xn_aggr[f][p], 1)
                v.wait_ge(xn_aggr[f][p], it + 1)
                nc.vector.tensor_scalar(var_eps[p][:], moments[p][:, :, 1], EPS, None,
                                        ALU.add).then_inc(var_ready[f][p], 1)

            def normalize(f, it, p):
                tile = it * 2 * TPC + p * TPC
                v.wait_ge(rstd_ready[f][p], it + 1)
                reached(v, tp_ready[f][p], it)
                for t in range(TPC):
                    ins = nc.vector.tensor_scalar(xn[p][:, t, :], x_sb[:, ds(tile + t, 1), :].rearrange("p a c -> p (a c)"),
                                                  moments[p][:, t, 0:1], rstd[p][:, t:t + 1],
                                                  ALU.subtract, ALU.mult)
                ins.then_inc(xn_ready[f][p], 1)

            def store_gates(f, it, p):
                reached(v, gate_ready[f][p], it + 1)
                nc.vector.tensor_tensor(gates[:, ds(it * 2 * TPC + p * TPC, TPC), :],
                                        st_ps[p][:, 0:TPC * E].rearrange("p (t e) -> p t e", e=E),
                                        gb[:].rearrange("p (a e) -> p a e", a=1).broadcast_to([P, TPC, E]),
                                        ALU.add).then_inc(gate_used[f][p], 1)

            def one_hot_of_best(values, hot):
                wide = best[:].broadcast_to([P, N_TILE, E])
                ranks = rank[:].rearrange("p (a e) -> p a e", a=1).broadcast_to([P, N_TILE, E])
                link(nc.vector.tensor_reduce(best[:], values, AX.X, ALU.max))
                link(nc.vector.tensor_tensor(hot, values, wide, ALU.is_equal))
                link(nc.vector.tensor_tensor(hot, hot, ranks, ALU.mult))
                link(nc.vector.tensor_reduce(best[:], hot, AX.X, ALU.max))
                link(nc.vector.tensor_tensor(hot, hot, wide, ALU.is_equal))

            def expert_weights(f):
                for p in range(2):
                    reached(v, gate_used[f][p], PAIRS)
                one_hot_of_best(gates[:], first[:])
                link(nc.vector.scalar_tensor_tensor(out=gate_tmp[:], in0=first[:], scalar=-BIG, in1=gates[:],
                                                    op0=ALU.mult, op1=ALU.add))
                one_hot_of_best(gate_tmp[:], second[:])
                link(nc.vector.tensor_tensor(first[:], first[:], second[:], ALU.add))
                nc.vector.tensor_reduce(counts[:], first[:].rearrange("p t e -> p e t"), AX.X,
                                        ALU.add).then_inc(cnt_ready[f], 1)
                v.wait_ge(cnt_sum[f], 1)
                link(nc.vector.tensor_scalar(weight[:], st_ps[0][:, 0:E], 0.5 / (N_TOK * TOP_K), None, ALU.mult))
                link(nc.vector.tensor_tensor(neg_b[:], eb[:], weight[:], ALU.mult))
                link(nc.vector.tensor_reduce(b_sum[:], neg_b[:], AX.X, ALU.add))
                link(nc.vector.tensor_scalar(neg_b[:], neg_b[:], -1.0, None, ALU.mult))
                nc.vector.tensor_tensor(ews[:], ew[:], weight[:].rearrange("p (e a) -> p e a", a=1).broadcast_to(
                    [P, E, C]), ALU.mult).then_inc(ews_ready[f], 1)

            def experts(f):
                with v.Fori(0, PAIRS) as it:
                    for e in range(E):
                        for p in range(2):
                            i = 2 * (e % 2) + p
                            v.wait_ge(exp_ready[f][i], it * (E // 2) + e // 2 + 1)
                            if e == 0:
                                reached(v, back_ready[f][p], it)
                                nc.vector.tensor_scalar(acc[p][:], exp_ps[i][:], neg_b[:, 0:1], b_sum[:],
                                                        ALU.max, ALU.add).then_inc(exp_used[f][i], 1)
                            else:
                                reached(v, exp_used[f][2 * ((e - 1) % 2) + p], it * (E // 2) + (e - 1) // 2 + 1)
                                nc.vector.scalar_tensor_tensor(
                                    out=acc[p][:], in0=exp_ps[i][:], scalar=neg_b[:, e:e + 1], in1=acc[p][:],
                                    op0=ALU.max, op1=ALU.add).then_inc(exp_used[f][i], 1)
                    for p in range(2):
                        reached(v, back_ready[f][p], it + 1)
                        tiles = x_sb[:, ds(it * 2 * TPC + p * TPC, TPC), :]
                        nc.vector.tensor_tensor(tiles, tiles, work[p][:].rearrange("p (t c) -> p t c", c=C),
                                                ALU.add).then_inc(x_done[f][p], 1)

            nc.vector.memset(pmax[:], -BIG)
            v.wait_ge(w_loaded, 16 * 20)
            for n in "qk":
                even, odd = up[n][:, 0, :, DHE:DH:2], up[n][:, 0, :, DHE + 1:DH:2]
                nc.vector.tensor_scalar(up[n][:, 1, :, DHE:DH:2], odd, -1.0, None, ALU.mult).then_inc(rot_w, 1)
                nc.vector.tensor_copy(up[n][:, 1, :, DHE + 1:DH:2], even).then_inc(rot_w, 1)
            v.wait_ge(w_prod, 3)
            for n, ps in (("q", bank[0]), ("k", bank[1])):
                src = ps[:, 0:H * DH * 2].rearrange("p (g m r i d) -> p g m r i d", g=G, m=2, r=2, i=2)
                for r in range(2):
                    for g in range(G):
                        for m in range(2):
                            nc.vector.tensor_copy(w_qk[n][:, r, g, :, 2 * m:2 * m + 2],
                                                  src[:, g, m, r, :, :].rearrange("p i d -> p d i"))
            nc.vector.tensor_copy(w_v[:], work[0][:, 0:C]).then_inc(w_ready, 1)

            v.wait_ge(consts, 11)
            v.wait_ge(x_loaded, 16 * B)
            with v.Fori(0, PAIRS) as it:
                for p in range(2):
                    statistics(0, it, p)
                for p in range(2):
                    normalize(0, it, p)
                for p in range(2):
                    store_gates(0, it, p)
            expert_weights(0)
            experts(0)

            for p in range(2):
                reached(v, x_done[0][p], PAIRS)
            with v.Fori(0, PAIRS) as it:
                for p in range(2):
                    statistics(1, it, p)
                for p in range(2):
                    normalize(1, it, p)
                for p in range(2):
                    n = 2 * it + p
                    for s in range(2):
                        reached(v, lo_ready, 2 * n)
                        for r, (dst, table) in enumerate(((rot_a, cos_sb), (rot_b, sin_sb))):
                            i = 2 * s + r
                            v.wait_ge(qk_ready[i], n + 1)
                            nc.vector.tensor_tensor(dst[:, s, :], qk_ps[i], table[:, p * CH:(p + 1) * CH],
                                                    ALU.mult).then_inc(rotated, 1)

            def maxima_unit(n, u):
                j, pieces = MAX_UNITS[u]
                w = u % 2
                v.wait_ge(unit_ready[w], (N_UNIT // 2) * n + u // 2 + 1)
                if pieces is None:
                    rows = work[w][0:2 * KT, 0:P]
                    atleast(v, m_loaded, 4 * 16 * n)
                    nc.vector.tensor_copy(m_parts[j][:, 0, :], rows).then_inc(m_hi, 1)
                    v.wait_ge(m_hi, 2 * n + j + 1)
                    nc.vector.tensor_tensor(m_parts[j][:, 1, :], rows, m_parts[j][:, 0, :],
                                            ALU.subtract).then_inc(unit_used[w], 1)
                    return
                col = 0
                for qt, k0, tiles in pieces:
                    piece = work[w][:, col:col + tiles * P]
                    col += tiles * P
                    if k0 == qt:
                        apart(v, dve_passed)
                        ins = nc.vector.tensor_tensor_reduce(junk[:, w, qt % 4, :], piece, causal[:], 1.0, -BIG, ALU.add,
                                                             ALU.max, pmax[:, j, qt, 0:1])
                    else:
                        ins = nc.vector.tensor_reduce(pmax[:, j, qt, 1 + k0 // 4:2 + k0 // 4], piece, AX.X, ALU.max)
                ins.then_inc(unit_used[w], 1)
                if u + 1 < N_UNIT and MAX_UNITS[u + 1][1] is None:
                    h = j // 2
                    for r in range(2):
                        k = (u - r) // 2 + 1
                        v.wait_ge(unit_used[(u - r) % 2], (N_UNIT // 2) * n + k)
                    nc.vector.tensor_reduce(neg_max[:, h * 2 * KT:(h + 1) * 2 * KT],
                                            pmax[:, 2 * h:2 * h + 2, :, :].rearrange("p j k c -> p (j k) c"),
                                            AX.X, ALU.max, negate=True).then_inc(neg_max_ready, 1)

            def copy_outputs(n, p, turn):
                v.wait_ge(pv_done, N_BATCH * n + N_BATCH)
                reached(v, y_written[p], 16 * 2 * HG * turn)
                for h in range(2):
                    nc.vector.tensor_copy(y_sb[p][:, h * CH:(h + 1) * CH], y_ps[h][:]).then_inc(y_copied, 1)

            for u in range(N_UNIT):
                maxima_unit(0, u)

            def group(n, p, turn, last=False, first=False):
                for u in range(N_UNIT if not last else 0):
                    if u == 0 and not first:
                        copy_outputs(n - 1, 1 - p, turn + p - 1)
                    maxima_unit(n + 1, u)
                if last:
                    copy_outputs(n - 1, 1 - p, turn + p - 1)
                    copy_outputs(n, p, turn)

            group(0, 0, 0, first=True)
            with v.Fori(0, N_GROUP // 2 - 1) as it:
                group(2 * it + 1, 1, it)
                group(2 * it + 2, 0, it + 1)
            group(N_GROUP - 1, 1, N_GROUP // 2 - 1, last=True)

            with v.Fori(0, PAIRS) as it:
                for p in range(2):
                    v.wait_ge(y_loaded[p], 32 * it + 32)
                    nc.vector.reciprocal(den_t[p], den_t[p]).then_inc(y_recip[p], 1)
                for p in range(2):
                    reached(v, attn_ready[p], it + 1)
                    tiles = x_sb[:, ds(it * 2 * TPC + p * TPC, TPC), :]
                    nc.vector.tensor_tensor(tiles, tiles, bank[p][:].rearrange("p (t c) -> p t c", c=C),
                                            ALU.add).then_inc(attn_added[p], 1)
                for p in range(2):
                    reached(v, attn_added[p], it + 1)
                    apart(v, dve_passed)
                    statistics(2, it, p)
                for p in range(2):
                    normalize(2, it, p)
                for p in range(2):
                    store_gates(2, it, p)
            expert_weights(2)
            experts(2)

        @block.tensor
        def _(pe):
            def transpose_chunk(f, it, p):
                pe.wait_ge(xn_ready[f][p], it + 1)
                reached(pe, xnt_ready[f][p], it)
                for t in range(TPC):
                    ins = nc.tensor.transpose(work[p][:, t * P:(t + 1) * P], xn[p][:, t, :], ident[:])
                ins.then_inc(tp_ready[f][p], 1)

            def gate_products(f, it, p):
                reached(pe, xnt_ready[f][p], it + 1)
                reached(pe, gate_used[f][p], it)
                for t in range(TPC):
                    ins = nc.tensor.matmul(st_ps[p][:, t * E:(t + 1) * E], xnt[p][:, t * P:(t + 1) * P], gw[:],
                                           start=True, stop=True)
                ins.then_inc(gate_ready[f][p], 1)

            def experts(f):
                pe.wait_ge(cnt_ready[f], 1)
                nc.tensor.matmul(st_ps[0][:, 0:E], ones[:], counts[:], start=True, stop=True).then_inc(cnt_sum[f], 1)
                pe.wait_ge(ews_ready[f], 1)
                for p in range(2):
                    reached(pe, xnt_saved[f][p], PAIRS)
                with pe.Fori(0, PAIRS) as it:
                    for e in range(E):
                        for p in range(2):
                            i = 2 * (e % 2) + p
                            reached(pe, exp_used[f][i], it * (E // 2) + e // 2)
                            nc.tensor.matmul(exp_ps[i][:], ews[:, e, :], xnt_all[:, ds(it * 2 * CH + p * CH, CH)],
                                             start=True, stop=True).then_inc(exp_ready[f][i], 1)
                    for p in range(2):
                        reached(pe, exp_used[f][2 + p], it * (E // 2) + E // 2)
                        reached(pe, x_done[f][p], it)
                        for t in range(TPC):
                            ins = nc.tensor.transpose(work[p][:, t * P:(t + 1) * P], acc[p][:, t * P:(t + 1) * P],
                                                      ident[:])
                        ins.then_inc(back_ready[f][p], 1)

            pe.wait_ge(rot_w, 4)
            for n, ps in (("q", bank[0]), ("k", bank[1]), ("v", work[0])):
                width = 2 * DH * (1 if n == "v" else 2)
                for m in range(H // 2):
                    rhs = up[n][:].rearrange("p r i d -> p (r i d)")[:, 0:width]
                    ins = nc.tensor.matmul(ps[:, m * width:(m + 1) * width], down[n][:, m, :], rhs,
                                           start=True, stop=True)
                ins.then_inc(w_prod, 1)

            pe.wait_ge(consts, 11)
            pe.wait_ge(w_ready, 1)
            with pe.Fori(0, PAIRS) as it:
                for p in range(2):
                    transpose_chunk(0, it, p)
                for p in range(2):
                    gate_products(0, it, p)
            experts(0)

            for p in range(2):
                reached(pe, x_done[0][p], PAIRS)
            with pe.Fori(0, PAIRS) as it:
                for p in range(2):
                    transpose_chunk(1, it, p)
                for p in range(2):
                    n = 2 * it + p
                    reached(pe, xnt_ready[1][p], it + 1)
                    for i in range(4):
                        reached(pe, rotated, 4 * n)
                        nc.tensor.matmul(qk_ps[i], w_qk["qk"[i // 2]][:, i % 2, :, :, :].rearrange(
                            "p g d j -> p (g d j)"), xnt[p][:], start=True, stop=True).then_inc(qk_ready[i], 1)
                    reached(pe, v_used, n)
                    for t in range(TPC):
                        ins = nc.tensor.matmul(bank[0][:, t * P:(t + 1) * P], xnt[p][:, t * P:(t + 1) * P], w_v[:],
                                               start=True, stop=True)
                    ins.then_inc(v_ready[p], 1)

            def maxima_unit(n, p, turn, u):
                j, pieces = MAX_UNITS[u]
                w = u % 2
                if u == 0:
                    pe.wait_ge(stack_loaded[p], (turn + 1) * 16 * 2 * len(PRODUCTS))
                atleast(pe, unit_used[w], (N_UNIT // 2) * n + u // 2)
                if pieces is None:
                    pe.wait_ge(neg_max_ready, 2 * n + j + 1)
                    ins = nc.tensor.transpose(work[w][0:2 * KT, 0:P], neg_max[:, j * 2 * KT:(j + 1) * 2 * KT],
                                              ident[:])
                else:
                    col = 0
                    for qt, k0, tiles in pieces:
                        ins = nc.tensor.matmul(work[w][:, col:col + tiles * P],
                                               stack_q[p][0:M_ROW, j, qt * P:(qt + 1) * P],
                                               stack_k[p][0:M_ROW, j, k0 * P:(k0 + tiles) * P],
                                               start=True, stop=True)
                        col += tiles * P
                ins.then_inc(unit_ready[w], 1)

            def scores(n, p, s):
                atleast(pe, exp_done, N_SLOT * n + s - 1)
                for j, kt, off in SLOTS[s]:
                    col, q = off, kt * P
                    while q < T:
                        w = min(T - q, CH - col % CH)
                        ins = nc.tensor.matmul(st_ps[s % 2][:, col:col + w], stack_k[p][0:K_ALL, j, kt * P:(kt + 1) * P],
                                               stack_q[p][0:K_ALL, j, q:q + w], start=True, stop=True)
                        col, q = col + w, q + w
                ins.then_inc(st_ready, 1)

            def values(n, p, b, i):
                steps = value_steps(b)
                if i == 0:
                    pe.wait_ge(masked, N_SLOT * n + LAST_SLOT[b] + 1)
                if b == 0 and i == 0:
                    pe.wait_ge(v_st_ready, n + 1)
                    atleast(pe, y_copied, 2 * n)
                for j, kt, s, col, q, w in steps[i]:
                    h, q0 = q // CH, q % CH
                    ins = nc.tensor.matmul(y_ps[h][j * HROW:(j + 1) * HROW, q0:q0 + w], v_st[p][:, kt, j, :],
                                           prob[s % N_PBUF][:, col:col + w],
                                           start=(kt == 0), stop=False, skip_group_check=True)
                if i == len(steps) - 1:
                    ins.then_inc(pv_done, 1)

            def group(n, p, turn, first=False, last=False):
                todo = {s: [] for s in range(N_SLOT)}
                for b in range(N_BATCH - 2):
                    for i in range(len(value_steps(b))):
                        todo[min(LAST_SLOT[b] + 2 + i, N_SLOT - 1)].append((b, i))
                u = 0
                for s in range(N_SLOT):
                    if s == 0:
                        pe.wait_ge(m_loaded, 4 * 16 * n + 4 * 16)
                    scores(n, p, s)
                    if s == 1 and not first:
                        tail(n - 1, 1 - p)
                    for b, i in todo[s]:
                        values(n, p, b, i)
                    if not last and s >= 4:
                        for _ in range(3):
                            if u < N_UNIT:
                                maxima_unit(n + 1, 1 - p, turn + p, u)
                                u += 1

            def tail(n, p):
                for b in range(N_BATCH - 2, N_BATCH):
                    for i in range(len(value_steps(b))):
                        values(n, p, b, i)

            reached(pe, rotated, 8 * PAIRS)
            reached(pe, v_used, 2 * PAIRS)
            for u in range(N_UNIT):
                maxima_unit(0, 0, 0, u)
            group(0, 0, 0, first=True)
            with pe.Fori(0, N_GROUP // 2 - 1) as it:
                group(2 * it + 1, 1, it)
                group(2 * it + 2, 0, it + 1)
            group(N_GROUP - 1, 1, N_GROUP // 2 - 1, last=True)
            tail(N_GROUP - 1, 1)

            with pe.Fori(0, PAIRS) as it:
                for p in range(2):
                    pe.wait_ge(y_norm[p], it + 1)
                    reached(pe, attn_added[p], it)
                    for t in range(TPC):
                        ins = nc.tensor.matmul(bank[p][:, t * P:(t + 1) * P], y_t[p][:, t * P:(t + 1) * P], wc_sb[:],
                                               start=True, stop=True)
                    ins.then_inc(attn_ready[p], 1)
                for p in range(2):
                    transpose_chunk(2, it, p)
                for p in range(2):
                    gate_products(2, it, p)
            experts(2)


def rotation_tables():
    inv_freq = np.float32(1.0) / np.float32(10000.0) ** (np.arange(0, DHE, 2, dtype=np.float32) / np.float32(DHE))
    freqs = np.arange(T, dtype=np.float32)[:, None] * inv_freq[None, :]
    emb = np.concatenate((freqs, freqs), axis=-1)
    dim = (np.arange(P) // HG) % DH
    cos, sin = np.ones((P, T), np.float32), np.zeros((P, T), np.float32)
    for d in range(DHE, DH):
        cos[dim == d] = np.cos(emb[:, d - DHE])
        sin[dim == d] = np.sin(emb[:, d - DHE])
    return cos, sin


def kernel(L0_attn_x, L0_attn_Wq_down, L0_attn_Wk_down, L0_attn_Wv_down, L0_attn_Wq_up_c, L0_attn_Wq_up_e,
           L0_attn_Wk_up_c, L0_attn_Wk_up_e, L0_attn_Wv_up, L0_attn_Wc, L0_ffn_gate_w, L0_ffn_gate_b,
           L0_ffn_expert_w, L0_ffn_expert_b):
    import concourse.bacc as bacc
    from concourse.bass_utils import run_bass_kernel_spmd

    def lay(a):
        return np.ascontiguousarray(a)

    def down_rows(w):
        return lay(np.asarray(w).T.reshape(H // 2, 2 * L, C).transpose(1, 0, 2))

    cos, sin = rotation_tables()
    arrays = {
        "x": lay(np.asarray(L0_attn_x).reshape(N_TOK, C)),
        "wq_t": down_rows(L0_attn_Wq_down), "wk_t": down_rows(L0_attn_Wk_down), "wv_t": down_rows(L0_attn_Wv_down),
        "q_c": lay(L0_attn_Wq_up_c), "q_e": lay(L0_attn_Wq_up_e),
        "k_c": lay(L0_attn_Wk_up_c), "k_e": lay(L0_attn_Wk_up_e),
        "v_up": lay(L0_attn_Wv_up), "wc": lay(L0_attn_Wc),
        "gate_wt": lay(np.asarray(L0_ffn_gate_w).T), "gate_b": lay(L0_ffn_gate_b),
        "exp_wt": lay(np.asarray(L0_ffn_expert_w).transpose(2, 0, 1)),
        "exp_bt": lay(np.asarray(L0_ffn_expert_b).T),
        "cos": cos, "sin": sin,
    }
    nc = bacc.Bacc("TRN2", target_bir_lowering=False, num_devices=1)
    ins = {n: nc.dram_tensor(n, a.shape, mybir.dt.from_np(a.dtype), kind="ExternalInput").ap()
           for n, a in arrays.items()}
    out = nc.dram_tensor("out", (N_TOK, C), F32, kind="ExternalOutput").ap()
    build(nc, **ins, out=out)
    result = run_bass_kernel_spmd(nc, [arrays], core_ids=[0])
    return result.results[0]["out"].reshape(B, T, C)
```

```python
from contextlib import ExitStack

import concourse.bass as bass
import numpy as np
from concourse import mybir

F32 = mybir.dt.float32
BF16 = mybir.dt.bfloat16
ALU = mybir.AluOpType
ACT = mybir.ActivationFunctionType
AX = mybir.AxisListType
ds = bass.ds

P = 128
B, T, C = 4, 1024, 128
H, L, DH = 16, 64, 8
DHE = DH // 2
E = 8
TOP_K = 2
N_TOK = B * T
N_TILE = N_TOK // P
CH = 512
TPC = CH // P
PAIRS = N_TOK // (2 * CH)
EPS = 1e-5
BIG = 3.0e38

HG = 4
G = H // HG
N_GROUP = B * G
KT = T // P
SCALE = 1.0 / float(np.sqrt(DH))
HROW = 32
PRODUCTS = [(0, 0), (0, 1), (0, 2), (1, 0), (1, 1), (2, 0)]
M_ROW = 96
LOOPS = 4
N_RING = 3

KINDS = [[(0, 0, CH)], [(0, CH, CH)]]
for _k in range(1, KT // 2):
    KINDS += [[(_k, _k * P, CH - _k * P), (KT - _k, T - _k * P, _k * P)], [(_k, CH, CH)]]
KINDS += [[(KT // 2, CH, CH)]]
N_BATCH = len(KINDS)
N_SLOT = N_BATCH * HG
N_PBUF = 3 * HG


def diagonals(kind):
    cols, col = [], 0
    for kt, q, w in KINDS[kind]:
        if q == kt * P:
            cols.append(col)
        col += w
    return cols


MASKED = [b for b in range(N_BATCH) if diagonals(b)]

MAX_UNITS = []
for _j in range(HG):
    MAX_UNITS += [(_j, [(qt, qt, 1) for qt in range(4)]), (_j, [(qt, qt, 1) for qt in range(4, 8)])]
    MAX_UNITS += [(_j, u) for u in (
        [(7, 0, 4)], [(7, 4, 3), (1, 0, 1)], [(6, 0, 4)], [(6, 4, 2), (2, 0, 2)],
        [(5, 0, 4)], [(5, 4, 1), (3, 0, 3)], [(4, 0, 4)])]
    if _j % 2:
        MAX_UNITS.append((_j // 2, None))
N_UNIT = len(MAX_UNITS)
LAG = HG + 2
AHEAD = 8


def units_beside(n_next, n_after, s):
    todo = [(n_next, u) for u in range(AHEAD, N_UNIT)] + [(n_after, u) for u in range(AHEAD)]
    lo, hi = s * N_UNIT // N_SLOT, (s + 1) * N_UNIT // N_SLOT
    return todo[lo:hi]


def atleast(eng, sem, value):
    if isinstance(value, int) and value <= 0:
        return
    eng.wait_ge(sem, value)


def reached(eng, sem, count):
    eng.wait_ge(sem, count + 1)


def apart(eng, passed):
    eng.sem_inc(passed, 1)


def build(nc, x, wq_t, wk_t, wv_t, q_c, q_e, k_c, k_e, v_up, wc, gate_wt, gate_b, exp_wt, exp_bt,
          cos, sin, out):
    ctx = ExitStack()
    with ctx:
        def sb(name, shape, dt=F32):
            return ctx.enter_context(nc.sbuf_tensor(name, shape, dt))

        def sem(name):
            return ctx.enter_context(nc.semaphore(name))

        def sem2(name):
            return [sem(f"{name}{p}") for p in range(2)]

        bank = [ctx.enter_context(nc.psum_tensor(f"bank{i}", [P, CH], F32)) for i in range(8)]
        y_ps = bank[0:2]
        st_ps = bank[2:5]
        work = bank[5:8]
        qk_ps = [bank[i][:] for i in (2, 3, 4, 7)]
        exp_ps = [bank[0], bank[1], bank[2], bank[3]]
        v_ps = bank[0]

        x_sb = sb("x_sb", [P, N_TILE, C])
        xnt_all = sb("xnt_all", [P, N_TOK])
        ident = sb("ident", [P, P])
        causal = sb("causal", [P, P])
        ones = sb("ones", [P, P])
        neg_half = sb("neg_half", [P, TPC])
        rank = sb("rank", [P, E])
        gw = sb("gw", [P, E])
        gb = sb("gb", [P, E])
        ew = sb("ew", [P, E, C])
        eb = sb("eb", [P, E])
        ews = sb("ews", [P, E, C])
        weight = sb("weight", [P, E])
        neg_b = sb("neg_b", [P, E])
        b_sum = sb("b_sum", [P, 1])
        up = {n: sb(f"up_{n}", [P, 2, 2, DH]) for n in "qkv"}
        w_qk = {n: sb(f"w_{n}", [P, 2, G, DH, HG]) for n in "qk"}
        w_v = sb("w_v", [P, C])
        wc_sb = sb("wc_sb", [P, C])
        stats = [sb(f"stats{p}", [P, TPC, 6]) for p in range(2)]
        moments = [sb(f"moments{p}", [P, TPC, 2]) for p in range(2)]
        var_eps = [sb(f"var_eps{p}", [P, TPC]) for p in range(2)]
        rstd = [sb(f"rstd{p}", [P, TPC]) for p in range(2)]
        xn = [sb(f"xn{p}", [P, TPC, C]) for p in range(2)]
        xnt = [sb(f"xnt{p}", [P, CH]) for p in range(2)]
        acc = [sb(f"acc{p}", [P, CH]) for p in range(2)]
        gates = sb("gates", [P, N_TILE, E])
        gate_tmp = sb("gate_tmp", [P, N_TILE, E])
        first = sb("first", [P, N_TILE, E])
        second = sb("second", [P, N_TILE, E])
        best = sb("best", [P, N_TILE, 1])
        counts = sb("counts", [P, E])
        parts = [sb(f"parts{p}", [P, 2, 3, CH], BF16) for p in range(2)]
        v_all = sb("v_all", [P, B * G, KT, HG * DH])
        stack_q = [sb(f"stack_q{r}", [P, HG, T], BF16) for r in range(N_RING)]
        stack_k = [sb(f"stack_k{r}", [P, HG, T], BF16) for r in range(N_RING)]
        v_st = [sb(f"v_st{r}", [P, KT, HG, HROW]) for r in range(N_RING)]
        prob = sb("prob", [P, N_PBUF, CH])
        down = {n: prob[:, 2 * i:2 * i + 2, :].rearrange("p a (m c) -> p (a m) c", c=C) for i, n in enumerate("qkv")}
        rot_a, rot_b, rest = (prob[:, 2 * i:2 * i + 2, :] for i in range(3))
        cos_sb, sin_sb = (prob[:, 2 * i:2 * i + 2, :].rearrange("p a t -> p (a t)") for i in (3, 4))
        pmax = sb("pmax", [P, HG, KT, 3])
        neg_max = sb("neg_max", [P, HG * KT])
        junk = sb("junk", [P, N_RING, 4, P])
        m_parts = [sb(f"m_parts{h}", [2 * KT, 2, P], BF16) for h in range(2)]
        y_sb = [sb(f"y_sb{r}", [P, T]) for r in range(N_RING)]
        y_t = [y_sb[p][:, 0:CH] for p in range(2)]
        den_t = [y_sb[p][:, CH:T] for p in range(2)]

        parts_dram = nc.dram_tensor("parts_dram", [2, 3, B, P, T], BF16, kind="Internal").ap()
        y_dram = nc.dram_tensor("y_dram", [N_GROUP, HG, 2, DH, T], F32, kind="Internal").ap()
        zero_dram = nc.dram_tensor("zero_dram", [2, HG, T], BF16, kind="Internal").ap()
        parts_by_group = parts_dram.rearrange("s c b (g f) t -> s c (b g) f t", g=G)

        x_loaded = sem("x_loaded")
        w_loaded = sem("w_loaded")
        pool_zeroed = sem("pool_zeroed")
        consts = sem("consts")
        dve_passed, pool_passed, sp_passed = sem("dve_passed"), sem("pool_passed"), sem("sp_passed")
        rot_w = sem("rot_w")
        w_prod = sem("w_prod")
        w_ready = sem("w_ready")
        dve = sem("dve")
        xn_stat = {f: sem2(f"xn_stat_{f}") for f in range(3)}
        xn_aggr = {f: sem2(f"xn_aggr_{f}") for f in range(3)}
        var_ready = {f: sem2(f"var_ready_{f}") for f in range(3)}
        rstd_ready = {f: sem2(f"rstd_ready_{f}") for f in range(3)}
        xn_ready = {f: sem2(f"xn_ready_{f}") for f in range(3)}
        tp_ready = {f: sem2(f"tp_ready_{f}") for f in range(3)}
        xnt_ready = {f: sem2(f"xnt_ready_{f}") for f in range(3)}
        xnt_saved = {f: sem2(f"xnt_saved_{f}") for f in (0, 2)}
        gate_ready = {f: sem2(f"gate_ready_{f}") for f in (0, 2)}
        gate_used = {f: sem2(f"gate_used_{f}") for f in (0, 2)}
        cnt_ready = {f: sem(f"cnt_ready_{f}") for f in (0, 2)}
        cnt_sum = {f: sem(f"cnt_sum_{f}") for f in (0, 2)}
        ews_ready = {f: sem(f"ews_ready_{f}") for f in (0, 2)}
        exp_ready = {f: [sem(f"exp_ready_{f}_{i}") for i in range(4)] for f in (0, 2)}
        exp_used = {f: [sem(f"exp_used_{f}_{i}") for i in range(4)] for f in (0, 2)}
        back_ready = {f: sem2(f"back_ready_{f}") for f in (0, 2)}
        x_done = {f: sem2(f"x_done_{f}") for f in (0, 2)}
        out_written = sem("out_written")

        qk_ready = [sem(f"qk_ready{i}") for i in range(4)]
        qk_used = [sem(f"qk_used{i}") for i in range(4)]
        v_ready = sem2("v_ready")
        v_used = sem("v_used")
        rotated = sem("rotated")
        rot_sum = sem("rot_sum")
        hi_ready = sem("hi_ready")
        rest_ready = sem("rest_ready")
        mid_ready = sem("mid_ready")
        lo_ready = sem("lo_ready")
        parts_written = sem2("parts_written")

        stack_init = sem("stack_init")
        zeros_stored = sem("zeros_stored")
        stack_loaded = [sem(f"stack_loaded{r}") for r in range(N_RING)]
        v_st_ready = sem("v_st_ready")
        st_ready = sem("st_ready")
        exp_done = sem("exp_done")
        masked = sem("masked")
        pv_done = sem("pv_done")
        y_copied = sem("y_copied")
        y_written = [sem(f"y_written{r}") for r in range(N_RING)]
        unit_ready = sem("unit_ready")
        unit_used = sem("unit_used")
        neg_max_ready = sem("neg_max_ready")
        m_hi = sem("m_hi")
        m_loaded = sem("m_loaded")

        y_loaded = sem2("y_loaded")
        y_recip = sem2("y_recip")
        y_norm = sem2("y_norm")
        attn_ready = sem2("attn_ready")
        attn_added = sem2("attn_added")

        start_at_one = [lo_ready, rotated, v_used]
        for pair in (v_ready, parts_written, y_written, attn_ready, attn_added):
            start_at_one += pair
        for by_front in (tp_ready, xnt_ready, gate_ready, xnt_saved, gate_used, exp_used, back_ready, x_done):
            for several in by_front.values():
                start_at_one += several

        block = ctx.enter_context(nc.Block())

        @block.sync
        def _(sp):
            for b in range(B):
                sp.dma_start(x_sb[:, b * KT:(b + 1) * KT, :],
                             x[b * T:(b + 1) * T, :].rearrange("(t p) c -> p t c", p=P)).then_inc(x_loaded, 16)
            sp.dma_start(gw[:], gate_wt).then_inc(w_loaded, 16)
            sp.dma_start(gb[:], gate_b.rearrange("(a e) -> a e", a=1).broadcast_to([P, E])).then_inc(w_loaded, 16)
            sp.dma_start(ew[:], exp_wt).then_inc(w_loaded, 16)
            sp.dma_start(eb[:], exp_bt).then_inc(w_loaded, 16)
            for n, src in (("q", wq_t), ("k", wk_t), ("v", wv_t)):
                sp.dma_start(down[n], src).then_inc(w_loaded, 16)
            sp.dma_start(wc_sb[:], wc).then_inc(w_loaded, 16)
            sp.dma_start(cos_sb, cos).then_inc(w_loaded, 16)
            sp.dma_start(sin_sb, sin).then_inc(w_loaded, 16)
            sp.wait_ge(pool_zeroed, 3)
            for i in range(2):
                rows = slice(i * L, (i + 1) * L)
                sp.dma_start(up["v"][rows, 0, i, :], v_up).then_inc(w_loaded, 16)
                for n, c_part, e_part in (("q", q_c, q_e), ("k", k_c, k_e)):
                    sp.dma_start(up[n][rows, 0, i, 0:DHE], c_part).then_inc(w_loaded, 16)
                    sp.dma_start(up[n][rows, 0, i, DHE:DH], e_part).then_inc(w_loaded, 16)

            sp.wait_ge(stack_init, 15)
            sp.dma_start(zero_dram, stack_q[0][M_ROW:M_ROW + 2, :, :]).then_inc(zeros_stored, 16)

            with sp.Fori(0, PAIRS) as it:
                for p in range(2):
                    reached(sp, lo_ready, 2 * (2 * it + p) + 2)
                    for s in range(2):
                        sp.dma_start(
                            parts_dram[s, :, ds(it, 1), :, p * CH:(p + 1) * CH].rearrange("c a f t -> (a f) c t"),
                            parts[p][:, s, :, :]).then_inc(parts_written[p], 16)

            def load_stacks(n, r):
                for side, stack in ((0, stack_q[r]), (1, stack_k[r])):
                    rows = [parts_by_group[side, ab[side], ds(n, 1), :, :].rearrange(
                        "a (d j) t -> (a d) j t", j=HG) for ab in PRODUCTS]
                    for i, src in enumerate(rows):
                        sp.dma_start(stack[i * DH:(i + 1) * DH, :, :], src).then_inc(stack_loaded[r], 16)
                sp.dma_start(stack_q[r][M_ROW:M_ROW + 2, :, :], zero_dram).then_inc(stack_loaded[r], 16)

            def load_maxima(n, r, h):
                sp.wait_ge(unit_used, N_UNIT * n + MAX_UNITS.index((h, None)) + 1)
                for c in range(2):
                    sp.dma_start(stack_q[r][M_ROW + c:M_ROW + c + 1, 2 * h:2 * h + 2, :].rearrange(
                                     "a j (k t) -> a (j k) t", t=P),
                                 m_parts[h][:, c, :]).then_inc(m_loaded, 16)

            def store_y(n, r):
                sp.wait_ge(y_copied, 2 * n + 2)
                apart(sp, sp_passed)
                for j in range(HG):
                    sp.dma_start(y_dram[ds(n, 1), j, :, :, :].rearrange("a c r t -> (a c r) t"),
                                 y_sb[r][j * HROW:j * HROW + 2 * DH, :]).then_inc(y_written[r], 16)

            def group(n, r, first=False):
                r_next, r_after = (r + 1) % N_RING, (r + 2) % N_RING
                last = N_GROUP - 1 - n if isinstance(n, int) else N_GROUP
                if last >= 2:
                    atleast(sp, st_ready, N_SLOT * n)
                    load_stacks(n + 2, r_after)
                if not first:
                    store_y(n - 1, r_after)
                if last >= 1:
                    for h in range(2):
                        load_maxima(n + 1, r_next, h)

            for p in range(2):
                reached(sp, parts_written[p], 32 * PAIRS)
            sp.wait_ge(zeros_stored, 16)
            for n in range(2):
                load_stacks(n, n)
            for h in range(2):
                load_maxima(0, 0, h)
            group(0, 0, first=True)
            with sp.Fori(0, LOOPS) as it:
                for r in (1, 2, 3):
                    group(N_RING * it + r, r % N_RING)
            for n in range(N_RING * LOOPS + 1, N_GROUP):
                group(n, n % N_RING)
            store_y(N_GROUP - 1, (N_GROUP - 1) % N_RING)

            for r in range(N_RING):
                reached(sp, y_written[r], 16 * HG * len(range(r, N_GROUP, N_RING)))
            y_rows = y_dram.rearrange("(b g) j c r t -> c b (g j) r t", b=B)
            with sp.Fori(0, PAIRS) as it:
                for p in range(2):
                    reached(sp, attn_ready[p], it)
                    for c, tile in enumerate((y_t[p], den_t[p])):
                        sp.dma_start(tile, y_rows[c, ds(it, 1), :, :, p * CH:(p + 1) * CH].rearrange(
                            "a h r t -> (a h) r t")).then_inc(y_loaded[p], 16)

            with sp.Fori(0, PAIRS) as it:
                for p in range(2):
                    reached(sp, x_done[2][p], it + 1)
                    sp.dma_start(out[ds(it * 2 * CH + p * CH, CH), :].rearrange("(t p) c -> p t c", p=P),
                                 x_sb[:, ds(it * 2 * TPC + p * TPC, TPC), :]).then_inc(out_written, 16)
            sp.wait_ge(out_written, 16 * 2 * PAIRS)

        @block.gpsimd
        def _(pool):
            for n in "qkv":
                nc.gpsimd.memset(up[n][:], 0.0).then_inc(pool_zeroed, 1)
            nc.gpsimd.memset(ones[:], 1.0).then_inc(pool_zeroed, 1)
            nc.gpsimd.memset(junk[:, 0, 0, :], 0.0).then_inc(pool_zeroed, 1)
            nc.gpsimd.memset(neg_half[:], -0.5).then_inc(consts, 1)
            for e in range(E):
                nc.gpsimd.memset(rank[:, e:e + 1], float(E - e)).then_inc(consts, 1)
            pool.wait_ge(pool_zeroed, 5)
            nc.gpsimd.affine_select(out=ident[:], in_=ones[:], compare_op=ALU.is_equal, fill=0.0, base=0,
                                    pattern=[[-1, P]], channel_multiplier=1).then_inc(consts, 1)
            nc.gpsimd.affine_select(out=causal[:], in_=junk[:, 0, 0, :], compare_op=ALU.is_ge, fill=-BIG, base=0,
                                    pattern=[[-1, P]], channel_multiplier=1).then_inc(consts, 1)
            for r in range(N_RING):
                for tile in (stack_q[r], stack_k[r], v_st[r]):
                    nc.gpsimd.memset(tile[:], 0.0).then_inc(stack_init, 1)
            pool.wait_ge(stack_init, 9)
            for r in range(N_RING):
                nc.gpsimd.memset(v_st[r][:, :, :, DH:2 * DH], 1.0).then_inc(stack_init, 1)
            pool.wait_ge(stack_init, 12)
            for r in range(N_RING):
                nc.gpsimd.memset(stack_k[r][M_ROW:P, :, :], 1.0).then_inc(stack_init, 1)
            pool.wait_ge(stack_init, 15)

            def inverse_deviations(f, it, p):
                pool.wait_ge(var_ready[f][p], it + 1)
                nc.gpsimd.tensor_tensor(rstd[p][:], var_eps[p][:], neg_half[:], ALU.pow).then_inc(rstd_ready[f][p], 1)

            def save_transposed(f, it, p):
                reached(pool, xnt_ready[f][p], it + 1)
                nc.gpsimd.tensor_copy(xnt_all[:, ds(it * 2 * CH + p * CH, CH)], xnt[p][:]).then_inc(xnt_saved[f][p], 1)

            def ffn_front(f):
                with pool.Fori(0, PAIRS) as it:
                    for p in range(2):
                        inverse_deviations(f, it, p)
                    for p in range(2):
                        save_transposed(f, it, p)

            pool.wait_ge(consts, 11)
            ffn_front(0)

            with pool.Fori(0, PAIRS) as it:
                for p in range(2):
                    inverse_deviations(1, it, p)
                for p in range(2):
                    n = 2 * it + p
                    for s in range(2):
                        reached(pool, rotated, 4 * n + 2 * s + 2)
                        nc.gpsimd.tensor_tensor(rot_a[:, s, :], rot_a[:, s, :], rot_b[:, s, :],
                                                ALU.add).then_inc(rot_sum, 1)
                    for s in range(2):
                        pool.wait_ge(hi_ready, 2 * n + s + 1)
                        nc.gpsimd.tensor_tensor(rest[:, s, :], rot_a[:, s, :], parts[p][:, s, 0, :],
                                                ALU.subtract).then_inc(rest_ready, 1)
                    for s in range(2):
                        pool.wait_ge(mid_ready, 2 * n + s + 1)
                        nc.gpsimd.tensor_tensor(parts[p][:, s, 2, :], rest[:, s, :], parts[p][:, s, 1, :],
                                                ALU.subtract).then_inc(lo_ready, 1)

            def stage_values(n, r):
                atleast(pool, pv_done, N_BATCH * (n - 2))
                nc.gpsimd.tensor_copy(v_st[r][:, :, :, 0:DH], v_all[:, ds(n, 1), :, :].rearrange(
                    "p a k (j d) -> p (a k) j d", d=DH)).then_inc(v_st_ready, 1)

            def group(n, r, first=False):
                last = n == N_GROUP - 1 if isinstance(n, int) else False
                for b in MASKED:
                    atleast(pool, exp_done, N_SLOT * n + HG * (b + 1))
                    apart(pool, pool_passed)
                    i = HG * b % N_PBUF
                    for col in diagonals(b):
                        tiles = prob[:, i:i + HG, col:col + P]
                        ins = nc.gpsimd.affine_select(out=tiles, in_=tiles, compare_op=ALU.is_ge, fill=0.0, base=0,
                                                      pattern=[[0, HG], [1, P]], channel_multiplier=-1)
                    ins.then_inc(masked, 1)
                    if b == 4 and not last:
                        stage_values(n + 1, (r + 1) % N_RING)

            reached(pool, v_used, 2 * PAIRS)
            stage_values(0, 0)
            group(0, 0, first=True)
            with pool.Fori(0, LOOPS) as it:
                for r in (1, 2, 3):
                    group(N_RING * it + r, r % N_RING)
            for n in range(N_RING * LOOPS + 1, N_GROUP):
                group(n, n % N_RING)

            with pool.Fori(0, PAIRS) as it:
                for p in range(2):
                    pool.wait_ge(y_recip[p], it + 1)
                    nc.gpsimd.tensor_tensor(y_t[p], y_t[p], den_t[p], ALU.mult).then_inc(y_norm[p], 1)
                for p in range(2):
                    inverse_deviations(2, it, p)
                for p in range(2):
                    save_transposed(2, it, p)

        @block.scalar
        def _(act):
            for one in start_at_one:
                act.sem_inc(one, 1)

            def copy_transposed(f, it, p):
                reached(act, tp_ready[f][p], it + 1)
                if f == 1:
                    reached(act, v_ready[p], it)
                else:
                    reached(act, gate_ready[f][p], it)
                    reached(act, xnt_saved[f][p], it)
                nc.scalar.copy(xnt[p][:], work[p][:]).then_inc(xnt_ready[f][p], 1)

            def front(f):
                with act.Fori(0, PAIRS) as it:
                    for p in range(2):
                        copy_transposed(f, it, p)

            front(0)

            with act.Fori(0, PAIRS) as it:
                for p in range(2):
                    copy_transposed(1, it, p)
                for p in range(2):
                    n = 2 * it + p
                    for s in range(2):
                        act.wait_ge(rot_sum, 2 * n + s + 1)
                        reached(act, parts_written[p], 32 * it)
                        nc.scalar.copy(parts[p][:, s, 0, :], rot_a[:, s, :]).then_inc(hi_ready, 1)
                    reached(act, v_ready[p], it + 1)
                    nc.scalar.copy(v_all[:, ds(it * G, G), p * TPC:(p + 1) * TPC, :],
                                   v_ps[:].rearrange("p (k g f) -> p g k f", k=TPC, g=G)).then_inc(v_used, 1)
                    for s in range(2):
                        act.wait_ge(rest_ready, 2 * n + s + 1)
                        nc.scalar.copy(parts[p][:, s, 1, :], rest[:, s, :]).then_inc(mid_ready, 1)

            def copy_outputs(n, r, turn):
                act.wait_ge(pv_done, N_BATCH * n + N_BATCH)
                reached(act, y_written[r], 16 * HG * turn)
                for h in range(2):
                    nc.scalar.copy(y_sb[r][:, h * CH:(h + 1) * CH], y_ps[h][:]).then_inc(y_copied, 1)

            def group(n, r, turn, first=False):
                for s in range(N_SLOT):
                    act.wait_ge(st_ready, N_SLOT * n + s + 1)
                    if s % HG == 0:
                        atleast(act, pv_done, N_BATCH * n + s // HG + 1 - N_PBUF // HG)
                    nc.scalar.activation(prob[:, s % N_PBUF, :], st_ps[s % N_RING][:], ACT.Exp,
                                         scale=SCALE).then_inc(exp_done, 1)
                    if s == 4 and not first:
                        copy_outputs(n - 1, (r - 1) % N_RING, turn - (r == 0))

            group(0, 0, 0, first=True)
            with act.Fori(0, LOOPS) as it:
                for r in (1, 2, 3):
                    group(N_RING * it + r, r % N_RING, it + r // N_RING)
            for n in range(N_RING * LOOPS + 1, N_GROUP):
                group(n, n % N_RING, n // N_RING)
            copy_outputs(N_GROUP - 1, (N_GROUP - 1) % N_RING, (N_GROUP - 1) // N_RING)

            front(2)

        @block.vector
        def _(v):
            chain = [0]

            def link(ins):
                chain[0] += 1
                ins.then_inc(dve, 1)
                v.wait_ge(dve, chain[0])

            def statistics(f, it, p):
                tile = it * 2 * TPC + p * TPC
                for t in range(TPC):
                    ins = nc.vector.bn_stats(stats[p][:, t, :], x_sb[:, ds(tile + t, 1), :].rearrange("p a c -> p (a c)"))
                ins.then_inc(xn_stat[f][p], 1)
                v.wait_ge(xn_stat[f][p], it + 1)
                apart(v, dve_passed)
                for t in range(TPC):
                    ins = nc.vector.bn_aggr(moments[p][:, t, :], stats[p][:, t, :])
                ins.then_inc(xn_aggr[f][p], 1)
                v.wait_ge(xn_aggr[f][p], it + 1)
                nc.vector.tensor_scalar(var_eps[p][:], moments[p][:, :, 1], EPS, None,
                                        ALU.add).then_inc(var_ready[f][p], 1)

            def normalize(f, it, p):
                tile = it * 2 * TPC + p * TPC
                v.wait_ge(rstd_ready[f][p], it + 1)
                reached(v, tp_ready[f][p], it)
                for t in range(TPC):
                    ins = nc.vector.tensor_scalar(xn[p][:, t, :], x_sb[:, ds(tile + t, 1), :].rearrange("p a c -> p (a c)"),
                                                  moments[p][:, t, 0:1], rstd[p][:, t:t + 1],
                                                  ALU.subtract, ALU.mult)
                ins.then_inc(xn_ready[f][p], 1)

            def store_gates(f, it, p):
                reached(v, gate_ready[f][p], it + 1)
                nc.vector.tensor_tensor(gates[:, ds(it * 2 * TPC + p * TPC, TPC), :],
                                        st_ps[p][:, 0:TPC * E].rearrange("p (t e) -> p t e", e=E),
                                        gb[:].rearrange("p (a e) -> p a e", a=1).broadcast_to([P, TPC, E]),
                                        ALU.add).then_inc(gate_used[f][p], 1)

            def one_hot_of_best(values, hot):
                wide = best[:].broadcast_to([P, N_TILE, E])
                ranks = rank[:].rearrange("p (a e) -> p a e", a=1).broadcast_to([P, N_TILE, E])
                link(nc.vector.tensor_reduce(best[:], values, AX.X, ALU.max))
                link(nc.vector.tensor_tensor(hot, values, wide, ALU.is_equal))
                link(nc.vector.tensor_tensor(hot, hot, ranks, ALU.mult))
                link(nc.vector.tensor_reduce(best[:], hot, AX.X, ALU.max))
                link(nc.vector.tensor_tensor(hot, hot, wide, ALU.is_equal))

            def expert_weights(f):
                for p in range(2):
                    reached(v, gate_used[f][p], PAIRS)
                one_hot_of_best(gates[:], first[:])
                link(nc.vector.scalar_tensor_tensor(out=gate_tmp[:], in0=first[:], scalar=-BIG, in1=gates[:],
                                                    op0=ALU.mult, op1=ALU.add))
                one_hot_of_best(gate_tmp[:], second[:])
                link(nc.vector.tensor_tensor(first[:], first[:], second[:], ALU.add))
                nc.vector.tensor_reduce(counts[:], first[:].rearrange("p t e -> p e t"), AX.X,
                                        ALU.add).then_inc(cnt_ready[f], 1)
                v.wait_ge(cnt_sum[f], 1)
                link(nc.vector.tensor_scalar(weight[:], st_ps[0][:, 0:E], 0.5 / (N_TOK * TOP_K), None, ALU.mult))
                link(nc.vector.tensor_tensor(neg_b[:], eb[:], weight[:], ALU.mult))
                link(nc.vector.tensor_reduce(b_sum[:], neg_b[:], AX.X, ALU.add))
                link(nc.vector.tensor_scalar(neg_b[:], neg_b[:], -1.0, None, ALU.mult))
                nc.vector.tensor_tensor(ews[:], ew[:], weight[:].rearrange("p (e a) -> p e a", a=1).broadcast_to(
                    [P, E, C]), ALU.mult).then_inc(ews_ready[f], 1)

            def experts(f):
                with v.Fori(0, PAIRS) as it:
                    for e in range(E):
                        for p in range(2):
                            i = 2 * (e % 2) + p
                            v.wait_ge(exp_ready[f][i], it * (E // 2) + e // 2 + 1)
                            if e == 0:
                                reached(v, back_ready[f][p], it)
                                nc.vector.tensor_scalar(acc[p][:], exp_ps[i][:], neg_b[:, 0:1], b_sum[:],
                                                        ALU.max, ALU.add).then_inc(exp_used[f][i], 1)
                            else:
                                reached(v, exp_used[f][2 * ((e - 1) % 2) + p], it * (E // 2) + (e - 1) // 2 + 1)
                                nc.vector.scalar_tensor_tensor(
                                    out=acc[p][:], in0=exp_ps[i][:], scalar=neg_b[:, e:e + 1], in1=acc[p][:],
                                    op0=ALU.max, op1=ALU.add).then_inc(exp_used[f][i], 1)
                    for p in range(2):
                        reached(v, back_ready[f][p], it + 1)
                        tiles = x_sb[:, ds(it * 2 * TPC + p * TPC, TPC), :]
                        nc.vector.tensor_tensor(tiles, tiles, work[p][:].rearrange("p (t c) -> p t c", c=C),
                                                ALU.add).then_inc(x_done[f][p], 1)

            nc.vector.memset(pmax[:], -BIG)
            v.wait_ge(w_loaded, 16 * 20)
            for n in "qk":
                even, odd = up[n][:, 0, :, DHE:DH:2], up[n][:, 0, :, DHE + 1:DH:2]
                nc.vector.tensor_scalar(up[n][:, 1, :, DHE:DH:2], odd, -1.0, None, ALU.mult).then_inc(rot_w, 1)
                nc.vector.tensor_copy(up[n][:, 1, :, DHE + 1:DH:2], even).then_inc(rot_w, 1)
            v.wait_ge(w_prod, 3)
            for n, ps in (("q", bank[0]), ("k", bank[1])):
                src = ps[:, 0:H * DH * 2].rearrange("p (g m r i d) -> p g m r i d", g=G, m=2, r=2, i=2)
                for r in range(2):
                    for g in range(G):
                        for m in range(2):
                            nc.vector.tensor_copy(w_qk[n][:, r, g, :, 2 * m:2 * m + 2],
                                                  src[:, g, m, r, :, :].rearrange("p i d -> p d i"))
            nc.vector.tensor_copy(w_v[:], work[0][:, 0:C]).then_inc(w_ready, 1)

            v.wait_ge(consts, 11)
            v.wait_ge(x_loaded, 16 * B)
            with v.Fori(0, PAIRS) as it:
                for p in range(2):
                    statistics(0, it, p)
                for p in range(2):
                    normalize(0, it, p)
                for p in range(2):
                    store_gates(0, it, p)
            expert_weights(0)
            experts(0)

            for p in range(2):
                reached(v, x_done[0][p], PAIRS)
            with v.Fori(0, PAIRS) as it:
                for p in range(2):
                    statistics(1, it, p)
                for p in range(2):
                    normalize(1, it, p)
                for p in range(2):
                    n = 2 * it + p
                    for s in range(2):
                        reached(v, lo_ready, 2 * n)
                        for r, (dst, table) in enumerate(((rot_a, cos_sb), (rot_b, sin_sb))):
                            i = 2 * s + r
                            v.wait_ge(qk_ready[i], n + 1)
                            nc.vector.tensor_tensor(dst[:, s, :], qk_ps[i], table[:, p * CH:(p + 1) * CH],
                                                    ALU.mult).then_inc(rotated, 1)

            def maxima_unit(n, r, u):
                j, pieces = MAX_UNITS[u]
                w = (N_UNIT * r + u) % N_RING
                v.wait_ge(unit_ready, N_UNIT * n + u + 1)
                if pieces is None:
                    rows = work[w][0:2 * KT, 0:P]
                    atleast(v, m_loaded, 4 * 16 * n)
                    nc.vector.tensor_copy(m_parts[j][:, 0, :], rows).then_inc(m_hi, 1)
                    v.wait_ge(m_hi, 2 * n + j + 1)
                    nc.vector.tensor_tensor(m_parts[j][:, 1, :], rows, m_parts[j][:, 0, :],
                                            ALU.subtract).then_inc(unit_used, 1)
                    return
                col = 0
                for qt, k0, tiles in pieces:
                    piece = work[w][:, col:col + tiles * P]
                    col += tiles * P
                    if k0 == qt:
                        if qt % 4 == 0:
                            apart(v, dve_passed)
                        ins = nc.vector.tensor_tensor_reduce(junk[:, w, qt % 4, :], piece, causal[:], 1.0, -BIG,
                                                             ALU.add, ALU.max, pmax[:, j, qt, 0:1])
                    else:
                        ins = nc.vector.tensor_reduce(pmax[:, j, qt, 1 + k0 // 4:2 + k0 // 4], piece, AX.X, ALU.max)
                ins.then_inc(unit_used, 1)
                if MAX_UNITS[(u + 1) % N_UNIT][1] is None:
                    h = j // 2
                    v.wait_ge(unit_used, N_UNIT * n + u + 1)
                    nc.vector.tensor_reduce(neg_max[:, h * 2 * KT:(h + 1) * 2 * KT],
                                            pmax[:, 2 * h:2 * h + 2, :, :].rearrange("p j k c -> p (j k) c"),
                                            AX.X, ALU.max, negate=True).then_inc(neg_max_ready, 1)

            def group(n, r):
                for s in range(N_SLOT):
                    for d, u in units_beside(1, 2, s):
                        if not isinstance(n, int) or n + d < N_GROUP:
                            maxima_unit(n + d, (r + d) % N_RING, u)

            for u in range(N_UNIT + AHEAD):
                maxima_unit(u // N_UNIT, u // N_UNIT, u % N_UNIT)
            group(0, 0)
            with v.Fori(0, LOOPS) as it:
                for r in (1, 2, 3):
                    group(N_RING * it + r, r % N_RING)
            for n in range(N_RING * LOOPS + 1, N_GROUP):
                group(n, n % N_RING)

            with v.Fori(0, PAIRS) as it:
                for p in range(2):
                    v.wait_ge(y_loaded[p], 32 * it + 32)
                    nc.vector.reciprocal(den_t[p], den_t[p]).then_inc(y_recip[p], 1)
                for p in range(2):
                    reached(v, attn_ready[p], it + 1)
                    tiles = x_sb[:, ds(it * 2 * TPC + p * TPC, TPC), :]
                    nc.vector.tensor_tensor(tiles, tiles, bank[p][:].rearrange("p (t c) -> p t c", c=C),
                                            ALU.add).then_inc(attn_added[p], 1)
                for p in range(2):
                    reached(v, attn_added[p], it + 1)
                    apart(v, dve_passed)
                    statistics(2, it, p)
                for p in range(2):
                    normalize(2, it, p)
                for p in range(2):
                    store_gates(2, it, p)
            expert_weights(2)
            experts(2)

        @block.tensor
        def _(pe):
            def transpose_chunk(f, it, p):
                pe.wait_ge(xn_ready[f][p], it + 1)
                reached(pe, xnt_ready[f][p], it)
                for t in range(TPC):
                    ins = nc.tensor.transpose(work[p][:, t * P:(t + 1) * P], xn[p][:, t, :], ident[:])
                ins.then_inc(tp_ready[f][p], 1)

            def gate_products(f, it, p):
                reached(pe, xnt_ready[f][p], it + 1)
                reached(pe, gate_used[f][p], it)
                for t in range(TPC):
                    ins = nc.tensor.matmul(st_ps[p][:, t * E:(t + 1) * E], xnt[p][:, t * P:(t + 1) * P], gw[:],
                                           start=True, stop=True)
                ins.then_inc(gate_ready[f][p], 1)

            def experts(f):
                pe.wait_ge(cnt_ready[f], 1)
                nc.tensor.matmul(st_ps[0][:, 0:E], ones[:], counts[:], start=True, stop=True).then_inc(cnt_sum[f], 1)
                pe.wait_ge(ews_ready[f], 1)
                for p in range(2):
                    reached(pe, xnt_saved[f][p], PAIRS)
                with pe.Fori(0, PAIRS) as it:
                    for e in range(E):
                        for p in range(2):
                            i = 2 * (e % 2) + p
                            reached(pe, exp_used[f][i], it * (E // 2) + e // 2)
                            nc.tensor.matmul(exp_ps[i][:], ews[:, e, :], xnt_all[:, ds(it * 2 * CH + p * CH, CH)],
                                             start=True, stop=True).then_inc(exp_ready[f][i], 1)
                    for p in range(2):
                        reached(pe, exp_used[f][2 + p], it * (E // 2) + E // 2)
                        reached(pe, x_done[f][p], it)
                        for t in range(TPC):
                            ins = nc.tensor.transpose(work[p][:, t * P:(t + 1) * P], acc[p][:, t * P:(t + 1) * P],
                                                      ident[:])
                        ins.then_inc(back_ready[f][p], 1)

            pe.wait_ge(rot_w, 4)
            for n, ps in (("q", bank[0]), ("k", bank[1]), ("v", work[0])):
                width = 2 * DH * (1 if n == "v" else 2)
                for m in range(H // 2):
                    rhs = up[n][:].rearrange("p r i d -> p (r i d)")[:, 0:width]
                    ins = nc.tensor.matmul(ps[:, m * width:(m + 1) * width], down[n][:, m, :], rhs,
                                           start=True, stop=True)
                ins.then_inc(w_prod, 1)

            pe.wait_ge(consts, 11)
            pe.wait_ge(w_ready, 1)
            with pe.Fori(0, PAIRS) as it:
                for p in range(2):
                    transpose_chunk(0, it, p)
                for p in range(2):
                    gate_products(0, it, p)
            experts(0)

            for p in range(2):
                reached(pe, x_done[0][p], PAIRS)
            with pe.Fori(0, PAIRS) as it:
                for p in range(2):
                    transpose_chunk(1, it, p)
                for p in range(2):
                    n = 2 * it + p
                    reached(pe, xnt_ready[1][p], it + 1)
                    for i in range(4):
                        reached(pe, rotated, 4 * n)
                        nc.tensor.matmul(qk_ps[i], w_qk["qk"[i // 2]][:, i % 2, :, :, :].rearrange(
                            "p g d j -> p (g d j)"), xnt[p][:], start=True, stop=True).then_inc(qk_ready[i], 1)
                    reached(pe, v_used, n)
                    for t in range(TPC):
                        ins = nc.tensor.matmul(bank[0][:, t * P:(t + 1) * P], xnt[p][:, t * P:(t + 1) * P], w_v[:],
                                               start=True, stop=True)
                    ins.then_inc(v_ready[p], 1)

            def maxima_unit(n, r, turn, u):
                j, pieces = MAX_UNITS[u]
                w = (N_UNIT * r + u) % N_RING
                if u == 0:
                    pe.wait_ge(stack_loaded[r], 16 * (2 * len(PRODUCTS) + 1) * (turn + 1))
                atleast(pe, unit_used, N_UNIT * n + u + 1 - N_RING)
                if pieces is None:
                    pe.wait_ge(neg_max_ready, 2 * n + j + 1)
                    ins = nc.tensor.transpose(work[w][0:2 * KT, 0:P], neg_max[:, j * 2 * KT:(j + 1) * 2 * KT],
                                              ident[:])
                else:
                    col = 0
                    for qt, k0, tiles in pieces:
                        ins = nc.tensor.matmul(work[w][:, col:col + tiles * P],
                                               stack_q[r][:, j, qt * P:(qt + 1) * P],
                                               stack_k[r][:, j, k0 * P:(k0 + tiles) * P],
                                               start=True, stop=True)
                        col += tiles * P
                ins.then_inc(unit_ready, 1)

            def scores(n, r, s):
                atleast(pe, exp_done, N_SLOT * n + s + 1 - N_RING)
                j, col = s % HG, 0
                for kt, q, w in KINDS[s // HG]:
                    ins = nc.tensor.matmul(st_ps[s % N_RING][:, col:col + w], stack_k[r][:, j, kt * P:(kt + 1) * P],
                                           stack_q[r][:, j, q:q + w], start=True, stop=True)
                    col += w
                ins.then_inc(st_ready, 1)

            def values(n, r, b, i):
                if i == 0 and b in MASKED:
                    pe.wait_ge(masked, len(MASKED) * n + MASKED.index(b) + 1)
                elif i == 0:
                    pe.wait_ge(exp_done, N_SLOT * n + HG * (b + 1))
                if b == 0:
                    pe.wait_ge(v_st_ready, n + 1)
                    atleast(pe, y_copied, 2 * n)
                col = sum(w for _, _, w in KINDS[b][:i])
                kt, q, w = KINDS[b][i]
                for j in range(HG):
                    ins = nc.tensor.matmul(y_ps[q // CH][j * HROW:(j + 1) * HROW, q % CH:q % CH + w],
                                           v_st[r][:, kt, j, :], prob[:, (HG * b + j) % N_PBUF, col:col + w],
                                           start=(kt == 0), stop=False, skip_group_check=True)
                if i == len(KINDS[b]) - 1:
                    ins.then_inc(pv_done, 1)

            def group(n, r, turn, first=False):
                pe.wait_ge(m_loaded, 4 * 16 * n + 4 * 16)
                todo = {s: [] for s in range(N_SLOT)}
                for b in range(N_BATCH - 1):
                    for i in range(len(KINDS[b])):
                        todo[HG * b + LAG + 2 * i].append((b, i))
                for s in range(N_SLOT):
                    scores(n, r, s)
                    if s == LAG - HG and not first:
                        values(n - 1, (r - 1) % N_RING, N_BATCH - 1, 0)
                    for d, u in units_beside(1, 2, s):
                        if not isinstance(n, int) or n + d < N_GROUP:
                            maxima_unit(n + d, (r + d) % N_RING, turn + (r + d) // N_RING, u)
                    for b, i in todo[s]:
                        values(n, r, b, i)

            reached(pe, rotated, 8 * PAIRS)
            reached(pe, v_used, 2 * PAIRS)
            for u in range(N_UNIT + AHEAD):
                maxima_unit(u // N_UNIT, u // N_UNIT, 0, u % N_UNIT)
            group(0, 0, 0, first=True)
            with pe.Fori(0, LOOPS) as it:
                for r in (1, 2, 3):
                    group(N_RING * it + r, r % N_RING, it + r // N_RING)
            for n in range(N_RING * LOOPS + 1, N_GROUP):
                group(n, n % N_RING, n // N_RING)
            values(N_GROUP - 1, (N_GROUP - 1) % N_RING, N_BATCH - 1, 0)

            with pe.Fori(0, PAIRS) as it:
                for p in range(2):
                    pe.wait_ge(y_norm[p], it + 1)
                    reached(pe, attn_added[p], it)
                    for t in range(TPC):
                        ins = nc.tensor.matmul(bank[p][:, t * P:(t + 1) * P], y_t[p][:, t * P:(t + 1) * P], wc_sb[:],
                                               start=True, stop=True)
                    ins.then_inc(attn_ready[p], 1)
                for p in range(2):
                    transpose_chunk(2, it, p)
                for p in range(2):
                    gate_products(2, it, p)
            experts(2)


def rotation_tables():
    inv_freq = np.float32(1.0) / np.float32(10000.0) ** (np.arange(0, DHE, 2, dtype=np.float32) / np.float32(DHE))
    freqs = np.arange(T, dtype=np.float32)[:, None] * inv_freq[None, :]
    emb = np.concatenate((freqs, freqs), axis=-1)
    dim = (np.arange(P) // HG) % DH
    cos, sin = np.ones((P, T), np.float32), np.zeros((P, T), np.float32)
    for d in range(DHE, DH):
        cos[dim == d] = np.cos(emb[:, d - DHE])
        sin[dim == d] = np.sin(emb[:, d - DHE])
    return cos, sin


def kernel(L0_attn_x, L0_attn_Wq_down, L0_attn_Wk_down, L0_attn_Wv_down, L0_attn_Wq_up_c, L0_attn_Wq_up_e,
           L0_attn_Wk_up_c, L0_attn_Wk_up_e, L0_attn_Wv_up, L0_attn_Wc, L0_ffn_gate_w, L0_ffn_gate_b,
           L0_ffn_expert_w, L0_ffn_expert_b):
    import concourse.bacc as bacc
    from concourse.bass_utils import run_bass_kernel_spmd

    def lay(a):
        return np.ascontiguousarray(a)

    def down_rows(w):
        return lay(np.asarray(w).T.reshape(H // 2, 2 * L, C).transpose(1, 0, 2))

    cos, sin = rotation_tables()
    arrays = {
        "x": lay(np.asarray(L0_attn_x).reshape(N_TOK, C)),
        "wq_t": down_rows(L0_attn_Wq_down), "wk_t": down_rows(L0_attn_Wk_down), "wv_t": down_rows(L0_attn_Wv_down),
        "q_c": lay(L0_attn_Wq_up_c), "q_e": lay(L0_attn_Wq_up_e),
        "k_c": lay(L0_attn_Wk_up_c), "k_e": lay(L0_attn_Wk_up_e),
        "v_up": lay(L0_attn_Wv_up), "wc": lay(L0_attn_Wc),
        "gate_wt": lay(np.asarray(L0_ffn_gate_w).T), "gate_b": lay(L0_ffn_gate_b),
        "exp_wt": lay(np.asarray(L0_ffn_expert_w).transpose(2, 0, 1)),
        "exp_bt": lay(np.asarray(L0_ffn_expert_b).T),
        "cos": cos, "sin": sin,
    }
    nc = bacc.Bacc("TRN2", target_bir_lowering=False, num_devices=1)
    ins = {n: nc.dram_tensor(n, a.shape, mybir.dt.from_np(a.dtype), kind="ExternalInput").ap()
           for n, a in arrays.items()}
    out = nc.dram_tensor("out", (N_TOK, C), F32, kind="ExternalOutput").ap()
    build(nc, **ins, out=out)
    result = run_bass_kernel_spmd(nc, [arrays], core_ids=[0])
    return result.results[0]["out"].reshape(B, T, C)
```

```python
from contextlib import ExitStack

import concourse.bass as bass
import numpy as np
from concourse import mybir

F32 = mybir.dt.float32
BF16 = mybir.dt.bfloat16
ALU = mybir.AluOpType
ACT = mybir.ActivationFunctionType
AX = mybir.AxisListType
ds = bass.ds

P = 128
B, T, C = 4, 1024, 128
H, L, DH = 16, 64, 8
DHE = DH // 2
E = 8
TOP_K = 2
N_TOK = B * T
N_TILE = N_TOK // P
CH = 512
TPC = CH // P
PAIRS = N_TOK // (2 * CH)
EPS = 1e-5
BIG = 3.0e38

HG = 4
G = H // HG
N_GROUP = B * G
KT = T // P
SCALE = 1.0 / float(np.sqrt(DH))
HROW = 32
PRODUCTS = [(0, 0), (0, 1), (0, 2), (1, 0), (1, 1), (2, 0)]
M_ROW = 96
STACK_PARTS = [(first, side, [ab[side] for ab in PRODUCTS[first:first + n]])
               for first, n in ((0, 3), (3, 2), (5, 1)) for side in range(2)]
N_STACK_DMA = len(STACK_PARTS) + 1
LOOPS = 4
N_RING = 3

KINDS = [[(0, 0, CH)], [(0, CH, CH)]]
for _k in range(1, KT // 2):
    KINDS += [[(_k, _k * P, CH - _k * P), (KT - _k, T - _k * P, _k * P)], [(_k, CH, CH)]]
KINDS += [[(KT // 2, CH, CH)]]
N_BATCH = len(KINDS)
DEN_W = HG * T // P
N_SLOT = N_BATCH * HG
N_PBUF = 3 * HG


def diagonals(kind):
    cols, col = [], 0
    for kt, q, w in KINDS[kind]:
        if q == kt * P:
            cols.append(col)
        col += w
    return cols


MASKED = [b for b in range(N_BATCH) if diagonals(b)]

LAG = 2 * HG
LAST_VALUES = LAG - HG
Y_COPY_SLOTS = (1, LAG - 2)


def values_at(s):
    return [(b, i) for b in range(N_BATCH - 1) for i in range(len(KINDS[b]))
            if min(HG * b + LAG + 2 * i, N_SLOT - 1) == s]


OUTPUT_MASKS = [MASKED[0], *MASKED[2:B]]
OUTPUT_SLOTS = ((9, 11), (23, 25), (32, 34))


SCORE_UNITS = [(j, pieces) for j in range(HG) for pieces in (
    [(qt, qt, 1) for qt in range(4)], [(7, 0, 4)], [(1, 0, 1), (3, 2, 1), (5, 4, 1), (7, 6, 1)],
    [(6, 0, 4)], [(qt, qt, 1) for qt in range(4, 8)], [(6, 4, 2), (7, 4, 2)], [(2, 0, 2), (3, 0, 2)],
    [(5, 0, 4)], [(4, 0, 4)])]
HALF = len(SCORE_UNITS) // 2
UNITS = [(0, j, pieces) for j, pieces in SCORE_UNITS]
UNITS.insert(HALF + 2, (0, 0, None))
UNITS.insert(2, (-1, 1, None))
N_UNIT = len(UNITS)
TURN_0 = UNITS.index((0, 0, None))
TURN_1 = UNITS.index((-1, 1, None))
HALF_ENDS = [i for i, (_, j, pieces) in enumerate(UNITS) if pieces == [(4, 0, 4)] and j % 2]


def reduced_column(pieces):
    return {1: 2, 2: 3, 4: 1}[pieces[0][2]]


AHEAD = 10


def units_beside(s):
    todo = [(1, i) for i in range(AHEAD, N_UNIT)] + [(2, i) for i in range(AHEAD)]
    return todo[s * N_UNIT // N_SLOT:(s + 1) * N_UNIT // N_SLOT]


def in_range(n, i):
    return not isinstance(n, int) or 0 <= n + UNITS[i][0] < N_GROUP


def units_done(n, i):
    if n == 0 and i < TURN_1 if isinstance(n, int) else False:
        return i + 2
    if isinstance(n, int) and n == N_GROUP:
        return N_UNIT * n + i + 1 - TURN_1
    return N_UNIT * n + i + 1


def bank_free(n, i):
    if isinstance(n, int) and N_UNIT * n + i < N_RING:
        return 0
    if isinstance(n, int) and n == 0 and i - N_RING < TURN_1:
        return units_done(0, i - N_RING)
    return N_UNIT * n + i + 1 - N_RING


def atleast(eng, sem, value):
    if isinstance(value, int) and value <= 0:
        return
    eng.wait_ge(sem, value)


def reached(eng, sem, count):
    eng.wait_ge(sem, count + 1)


def apart(eng, passed):
    eng.sem_inc(passed, 1)


def build(nc, x, wq_t, wk_t, wv_t, q_c, q_e, k_c, k_e, v_up, wc, gate_wt, gate_b, exp_wt, exp_bt,
          cos, sin, out):
    ctx = ExitStack()
    with ctx:
        def sb(name, shape, dt=F32):
            return ctx.enter_context(nc.sbuf_tensor(name, shape, dt))

        def sem(name):
            return ctx.enter_context(nc.semaphore(name))

        def sem2(name):
            return [sem(f"{name}{p}") for p in range(2)]

        bank = [ctx.enter_context(nc.psum_tensor(f"bank{i}", [P, CH], F32)) for i in range(8)]
        y_ps = bank[0:2]
        st_ps = bank[2:5]
        work = bank[5:8]
        qk_ps = [bank[i][:] for i in (2, 3, 4, 7)]
        gate_ps = bank[4]
        exp_ps = [bank[0], bank[1], bank[2], bank[3]]
        v_ps = bank[0:2]
        w_prod_ps = {"q": bank[7][:, 0:CH // 2], "k": bank[7][:, CH // 2:CH], "v": bank[0][:, 0:C]}

        x_sb = sb("x_sb", [P, N_TILE, C])
        xnt_all = sb("xnt_all", [P, N_TOK])
        ident = sb("ident", [P, P])
        causal = sb("causal", [P, P])
        ones = sb("ones", [P, P])
        neg_half = sb("neg_half", [P, N_TILE])
        rank = sb("rank", [P, E])
        gw = sb("gw", [P, E])
        gb = sb("gb", [P, E])
        ew = sb("ew", [P, E, C])
        eb = sb("eb", [P, E])
        ews = sb("ews", [P, E, C])
        weight = sb("weight", [P, E])
        neg_b = sb("neg_b", [P, E])
        b_sum = sb("b_sum", [P, 1])
        up = {n: sb(f"up_{n}", [P, 2, 2, DH]) for n in "qkv"}
        w_qk = {n: sb(f"w_{n}", [P, 2, G, DH, HG]) for n in "qk"}
        w_v = sb("w_v", [P, C])
        wc_sb = sb("wc_sb", [P, C])
        stats = sb("stats", [P, N_TILE, 6])
        new_moments = sb("new_moments", [P, N_TILE, 2])
        means = sb("means", [P, N_TILE])
        var_eps = sb("var_eps", [P, N_TILE])
        rstd = sb("rstd", [P, N_TILE])
        xn = [sb(f"xn{p}", [P, TPC, C]) for p in range(2)]
        xnt = [sb(f"xnt{p}", [P, CH]) for p in range(2)]
        acc = [sb(f"acc{p}", [P, CH]) for p in range(2)]
        gates = sb("gates", [P, N_TILE, E])
        gate_tmp = sb("gate_tmp", [P, N_TILE, E])
        first = sb("first", [P, N_TILE, E])
        second = sb("second", [P, N_TILE, E])
        best = sb("best", [P, N_TILE, 1])
        counts = sb("counts", [P, E])
        parts = [sb(f"parts{p}", [P, 2, 3, CH], BF16) for p in range(2)]
        v_all = sb("v_all", [P, B * G, KT, HG * DH])
        stack_q = [sb(f"stack_q{r}", [P, HG, T], BF16) for r in range(N_RING)]
        stack_k = [sb(f"stack_k{r}", [P, HG, T], BF16) for r in range(N_RING)]
        v_st = [sb(f"v_st{r}", [P, KT, HG, HROW]) for r in range(N_RING)]
        prob = sb("prob", [P, N_PBUF, CH])
        down = {n: prob[:, 2 * i:2 * i + 2, :].rearrange("p a (m c) -> p (a m) c", c=C) for i, n in enumerate("qkv")}
        rot_a = [prob[:, 2 * i:2 * i + 2, :] for i in (0, 5)]
        rot_b, rest = (prob[:, 2 * i:2 * i + 2, :] for i in (1, 2))
        cos_sb, sin_sb = (prob[:, 2 * i:2 * i + 2, :].rearrange("p a t -> p (a t)") for i in (3, 4))
        den = sb("den", [P, DEN_W])
        rec = sb("rec", [P, DEN_W])
        pmax = sb("pmax", [P, HG, KT, 4])
        neg_max = sb("neg_max", [P, HG * KT])
        junk = sb("junk", [P, N_RING, 4, P])
        m_parts = [sb(f"m_parts{h}", [2 * KT, 2, P], BF16) for h in range(2)]
        y_sb = [sb(f"y_sb{r}", [P, T]) for r in range(N_RING)]

        free_r = (N_GROUP - 3) % N_RING
        y_t, rec_t = [y_sb[free_r][:, p * CH:(p + 1) * CH] for p in range(2)], acc

        parts_dram = nc.dram_tensor("parts_dram", [2, 3, B, P, T], BF16, kind="Internal").ap()
        y_dram = nc.dram_tensor("y_dram", [N_GROUP, HG, DH, T], F32, kind="Internal").ap()
        rec_dram = nc.dram_tensor("rec_dram", [N_GROUP, HG, T], F32, kind="Internal").ap()
        zero_dram = nc.dram_tensor("zero_dram", [2, HG, T], BF16, kind="Internal").ap()
        parts_by_group = parts_dram.rearrange("s c b (g f) t -> s c (b g) f t", g=G)

        x_loaded = sem("x_loaded")
        w_loaded = sem("w_loaded")
        pool_zeroed = sem("pool_zeroed")
        consts = sem("consts")
        dve_passed, pool_passed, sp_passed = sem("dve_passed"), sem("pool_passed"), sem("sp_passed")
        rot_w = sem("rot_w")
        w_prod = sem("w_prod")
        w_ready = sem("w_ready")
        dve = sem("dve")
        stat_ready = {f: sem(f"stat_ready_{f}") for f in range(3)}
        moments_ready = {f: sem(f"moments_ready_{f}") for f in range(3)}
        means_ready = {f: sem(f"means_ready_{f}") for f in range(3)}
        var_ready = {f: sem(f"var_ready_{f}") for f in range(3)}
        rstd_ready = {f: sem(f"rstd_ready_{f}") for f in range(3)}
        xn_ready = {f: sem2(f"xn_ready_{f}") for f in range(3)}
        tp_ready = {f: sem2(f"tp_ready_{f}") for f in range(3)}
        xnt_ready = {f: sem2(f"xnt_ready_{f}") for f in range(3)}
        xnt_saved = {f: sem2(f"xnt_saved_{f}") for f in (0, 2)}
        gates_ready = {f: sem2(f"gates_ready_{f}") for f in (0, 2)}
        cnt_ready = {f: sem(f"cnt_ready_{f}") for f in (0, 2)}
        cnt_sum = {f: sem(f"cnt_sum_{f}") for f in (0, 2)}
        ews_ready = {f: sem(f"ews_ready_{f}") for f in (0, 2)}
        exp_ready = {f: [sem(f"exp_ready_{f}_{i}") for i in range(4)] for f in (0, 2)}
        exp_used = {f: [sem(f"exp_used_{f}_{i}") for i in range(4)] for f in (0, 2)}
        back_ready = {f: sem2(f"back_ready_{f}") for f in (0, 2)}
        x_done = {f: sem2(f"x_done_{f}") for f in (0, 2)}
        out_written = sem("out_written")

        qk_ready = [sem(f"qk_ready{i}") for i in range(4)]
        qk_used = [sem(f"qk_used{i}") for i in range(4)]
        v_ready = sem2("v_ready")
        v_used = sem2("v_used")
        rot_sum = sem("rot_sum")
        hi_ready = sem("hi_ready")
        rest_ready = [sem(f"rest_ready{s}") for s in range(2)]
        mid_ready = sem("mid_ready")
        lo_ready = sem("lo_ready")
        parts_written = sem2("parts_written")

        stack_init = sem("stack_init")
        zeros_stored = sem("zeros_stored")
        stack_loaded = [sem(f"stack_loaded{r}") for r in range(N_RING)]
        v_st_ready = sem("v_st_ready")
        st_ready = sem("st_ready")
        exp_done = sem("exp_done")
        masked = sem("masked")
        pv_done = sem("pv_done")
        y_copied = sem("y_copied")
        y_written = [sem(f"y_written{r}") for r in range(N_RING)]
        den_loaded = sem("den_loaded")
        rec_ready = sem("rec_ready")
        rec_written = sem("rec_written")
        unit_ready = sem("unit_ready")
        unit_used = sem("unit_used")
        neg_max_ready = sem("neg_max_ready")
        m_hi = sem("m_hi")
        m_loaded = sem("m_loaded")

        y_loaded = sem2("y_loaded")
        y_norm = sem2("y_norm")
        attn_ready = sem2("attn_ready")
        attn_added = sem2("attn_added")

        start_at_one = [lo_ready, mid_ready, unit_ready, unit_used, *qk_used]
        for pair in (v_ready, v_used, y_loaded, y_norm, parts_written, y_written, attn_ready, attn_added):
            start_at_one += pair
        for by_front in (tp_ready, xnt_ready, xnt_saved, gates_ready, exp_used, back_ready, x_done):
            for several in by_front.values():
                start_at_one += several

        block = ctx.enter_context(nc.Block())

        @block.sync
        def _(sp):
            for b in range(B):
                sp.dma_start(x_sb[:, b * KT:(b + 1) * KT, :],
                             x[b * T:(b + 1) * T, :].rearrange("(t p) c -> p t c", p=P)).then_inc(x_loaded, 16)
            sp.dma_start(gw[:], gate_wt).then_inc(w_loaded, 16)
            sp.dma_start(gb[:], gate_b.rearrange("(a e) -> a e", a=1).broadcast_to([P, E])).then_inc(w_loaded, 16)
            sp.dma_start(ew[:], exp_wt).then_inc(w_loaded, 16)
            sp.dma_start(eb[:], exp_bt).then_inc(w_loaded, 16)
            for n, src in (("q", wq_t), ("k", wk_t), ("v", wv_t)):
                sp.dma_start(down[n], src).then_inc(w_loaded, 16)
            sp.dma_start(wc_sb[:], wc).then_inc(w_loaded, 16)
            sp.dma_start(cos_sb, cos).then_inc(w_loaded, 16)
            sp.dma_start(sin_sb, sin).then_inc(w_loaded, 16)
            sp.wait_ge(pool_zeroed, 3)
            for i in range(2):
                rows = slice(i * L, (i + 1) * L)
                sp.dma_start(up["v"][rows, 0, i, :], v_up).then_inc(w_loaded, 16)
                for n, c_part, e_part in (("q", q_c, q_e), ("k", k_c, k_e)):
                    sp.dma_start(up[n][rows, 0, i, 0:DHE], c_part).then_inc(w_loaded, 16)
                    sp.dma_start(up[n][rows, 0, i, DHE:DH], e_part).then_inc(w_loaded, 16)

            sp.wait_ge(stack_init, 15)
            sp.dma_start(zero_dram, stack_q[0][M_ROW:M_ROW + 2, :, :]).then_inc(zeros_stored, 16)

            def store_parts(it, p):
                reached(sp, lo_ready, 2 * (2 * it + p) + 2)
                for s in range(2):
                    sp.dma_start(
                        parts_dram[s, :, ds(it, 1), :, p * CH:(p + 1) * CH].rearrange("c a f t -> (a f) c t"),
                        parts[p][:, s, :, :]).then_inc(parts_written[p], 16)

            def load_stack_part(n, r, k):
                if k == N_STACK_DMA - 1:
                    sp.dma_start(stack_q[r][M_ROW:M_ROW + 2, :, :], zero_dram).then_inc(stack_loaded[r], 16)
                    return
                first, side, of = STACK_PARTS[k]
                stack = (stack_q[r], stack_k[r])[side]
                src = parts_by_group[side, of[0]:of[-1] + 1, ds(n, 1), :, :].rearrange("c a (d j) t -> c (a d) j t", j=HG)
                if of[0] == of[-1]:
                    src = src.broadcast_to([len(of), DH, HG, T])
                sp.dma_start(stack[first * DH:(first + len(of)) * DH, :, :], src).then_inc(stack_loaded[r], 16)

            def load_stacks(n, r):
                for k in range(N_STACK_DMA):
                    load_stack_part(n, r, k)

            def load_maxima(n, r, h):
                sp.wait_ge(unit_used, units_done(n, TURN_0) if h == 0 else units_done(n + 1, TURN_1))
                for c in range(2):
                    sp.dma_start(stack_q[r][M_ROW + c:M_ROW + c + 1, 2 * h:2 * h + 2, :].rearrange(
                                     "a j (k t) -> a (j k) t", t=P),
                                 m_parts[h][:, c, :]).then_inc(m_loaded, 16)

            def store_y(n, r):
                sp.wait_ge(y_copied, 2 * n + 2)
                apart(sp, sp_passed)
                atleast(sp, rec_ready, n)
                for j in range(HG):
                    sp.dma_start(den[j * HROW:(j + 1) * HROW, :],
                                 y_sb[r][j * HROW + DH:j * HROW + DH + 1, :].rearrange(
                                     "a (k e) -> a k e", e=DEN_W)).then_inc(den_loaded, 16)
                for j in range(HG):
                    sp.dma_start(y_dram[ds(n, 1), j, :, :].rearrange("a r t -> (a r) t"),
                                 y_sb[r][j * HROW:j * HROW + DH, :]).then_inc(y_written[r], 16)

            def store_reciprocals(n):
                sp.wait_ge(rec_ready, n + 1)
                apart(sp, sp_passed)
                sp.dma_start(rec_dram[ds(n, 1), :, :].rearrange("a j (k e) -> (a j k) e", e=DEN_W),
                             rec[:]).then_inc(rec_written, 16)

            y_rows = y_dram.rearrange("(b g) j r t -> b (g j r) t", b=B)
            rec_rows = rec_dram.rearrange("(b g) j t -> b (g j) t", b=B)

            def outputs_written(groups):
                sp.wait_ge(rec_written, 16 * groups)
                for r in range(N_RING):
                    reached(sp, y_written[r], 16 * HG * len(range(r, groups, N_RING)))

            def load_outputs(it):
                for p in range(2):
                    reached(sp, attn_ready[p], it)
                    sp.dma_start(y_t[p], y_rows[it, :, p * CH:(p + 1) * CH]).then_inc(y_loaded[p], 16)
                    reached(sp, y_norm[p], it)
                    sp.dma_start(rec_t[p][:], rec_rows[it:it + 1, :, p * CH:(p + 1) * CH].rearrange(
                        "a h t -> h a t").broadcast_to([H, DH, CH])).then_inc(y_loaded[p], 16)

            def group(n, r, first=False):
                r_next, r_after = (r + 1) % N_RING, (r + 2) % N_RING
                last = N_GROUP - 1 - n if isinstance(n, int) else N_GROUP
                if last == 0:
                    outputs_written((B - 1) * G)
                    reached(sp, y_written[free_r], 16 * HG * len(range(free_r, N_GROUP, N_RING)))
                    load_outputs(0)
                if last >= 2:
                    atleast(sp, st_ready, N_SLOT * n)
                    load_stacks(n + 2, r_after)
                if not first:
                    store_y(n - 1, r_after)
                if last >= 1:
                    load_maxima(n + 1, r_next, 0)
                if not first:
                    store_reciprocals(n - 1)
                if last >= 1:
                    load_maxima(n + 1, r_next, 1)
                if last == 0:
                    for it in range(1, B - 1):
                        load_outputs(it)

            for p in range(2):
                store_parts(0, p)
            for p in range(2):
                reached(sp, parts_written[p], 32)
            sp.wait_ge(zeros_stored, 16)
            loads = [(n, k) for n in range(2) for k in range(N_STACK_DMA)]
            later = 2 * (PAIRS - 1)
            for c in range(later):
                store_parts(1 + c // 2, c % 2)
                for n, k in loads[c * len(loads) // later:(c + 1) * len(loads) // later]:
                    load_stack_part(n, n, k)
            for p in range(2):
                reached(sp, parts_written[p], 32 * PAIRS)
            for h in range(2):
                load_maxima(0, 0, h)
            group(0, 0, first=True)
            with sp.Fori(0, LOOPS) as it:
                for r in (1, 2, 3):
                    group(N_RING * it + r, r % N_RING)
            for n in range(N_RING * LOOPS + 1, N_GROUP):
                group(n, n % N_RING)
            store_y(N_GROUP - 1, (N_GROUP - 1) % N_RING)
            store_reciprocals(N_GROUP - 1)
            outputs_written(N_GROUP)
            load_outputs(B - 1)

            with sp.Fori(0, PAIRS) as it:
                for p in range(2):
                    reached(sp, x_done[2][p], it + 1)
                    sp.dma_start(out[ds(it * 2 * CH + p * CH, CH), :].rearrange("(t p) c -> p t c", p=P),
                                 x_sb[:, ds(it * 2 * TPC + p * TPC, TPC), :]).then_inc(out_written, 16)
            sp.wait_ge(out_written, 16 * 2 * PAIRS)

        @block.gpsimd
        def _(pool):
            def inverse_deviations(f, count, first, tiles):
                pool.wait_ge(var_ready[f], count)
                nc.gpsimd.tensor_tensor(rstd[:, ds(first, tiles)], var_eps[:, ds(first, tiles)],
                                        neg_half[:, 0:tiles], ALU.pow).then_inc(rstd_ready[f], 1)

            for n in "qkv":
                nc.gpsimd.memset(up[n][:], 0.0).then_inc(pool_zeroed, 1)
            nc.gpsimd.memset(ones[:], 1.0).then_inc(pool_zeroed, 1)
            nc.gpsimd.memset(junk[:, 0, 0, :], 0.0).then_inc(pool_zeroed, 1)
            nc.gpsimd.memset(neg_half[:], -0.5).then_inc(consts, 1)
            for e in range(E):
                nc.gpsimd.memset(rank[:, e:e + 1], float(E - e)).then_inc(consts, 1)
            pool.wait_ge(pool_zeroed, 5)
            nc.gpsimd.affine_select(out=ident[:], in_=ones[:], compare_op=ALU.is_equal, fill=0.0, base=0,
                                    pattern=[[-1, P]], channel_multiplier=1).then_inc(consts, 1)
            nc.gpsimd.affine_select(out=causal[:], in_=junk[:, 0, 0, :], compare_op=ALU.is_ge, fill=-BIG, base=0,
                                    pattern=[[-1, P]], channel_multiplier=1).then_inc(consts, 1)
            pool.wait_ge(consts, 11)
            inverse_deviations(0, 1, 0, N_TILE)
            for r in range(N_RING):
                for tile in (stack_q[r], stack_k[r], v_st[r]):
                    nc.gpsimd.memset(tile[:], 0.0).then_inc(stack_init, 1)
            pool.wait_ge(stack_init, 9)
            for r in range(N_RING):
                nc.gpsimd.memset(v_st[r][:, :, :, DH:DH + 1], 1.0).then_inc(stack_init, 1)
            pool.wait_ge(stack_init, 12)
            for r in range(N_RING):
                nc.gpsimd.memset(stack_k[r][M_ROW:P, :, :], 1.0).then_inc(stack_init, 1)
            pool.wait_ge(stack_init, 15)

            with pool.Fori(0, PAIRS) as it:
                inverse_deviations(1, it + 1, it * 2 * TPC, 2 * TPC)

            def split(n, p):
                pool.wait_ge(hi_ready, 2 * n + 2)
                reached(pool, lo_ready, 2 * n)
                nc.gpsimd.tensor_tensor(rest[:, 1, :], rot_a[p][:, 1, :], parts[p][:, 1, 0, :],
                                        ALU.subtract).then_inc(rest_ready[1], 1)

            def split_last(n, p):
                for s in range(2):
                    reached(pool, mid_ready, 2 * n + s + 1)
                    nc.gpsimd.tensor_tensor(parts[p][:, s, 2, :], rest[:, s, :], parts[p][:, s, 1, :],
                                            ALU.subtract).then_inc(lo_ready, 1)

            with pool.Fori(0, PAIRS) as it:
                for p in range(2):
                    split(2 * it + p, p)
                    split_last(2 * it + p, p)

            def stage_values(n, r):
                atleast(pool, pv_done, N_BATCH * (n - 2))
                nc.gpsimd.tensor_copy(v_st[r][:, :, :, 0:DH], v_all[:, ds(n, 1), :, :].rearrange(
                    "p a k (j d) -> p (a k) j d", d=DH)).then_inc(v_st_ready, 1)

            def divide_outputs(it):
                for p in range(2):
                    reached(pool, y_loaded[p], 32 * (it + 1))
                    nc.gpsimd.tensor_tensor(y_t[p], y_t[p], rec_t[p][:], ALU.mult).then_inc(y_norm[p], 1)

            def group(n, r, first=False):
                last = n == N_GROUP - 1 if isinstance(n, int) else False
                for b in MASKED:
                    atleast(pool, exp_done, N_SLOT * n + HG * (b + 1))
                    apart(pool, pool_passed)
                    i = HG * b % N_PBUF
                    for col in diagonals(b):
                        tiles = prob[:, i:i + HG, col:col + P]
                        ins = nc.gpsimd.affine_select(out=tiles, in_=tiles, compare_op=ALU.is_ge, fill=0.0, base=0,
                                                      pattern=[[0, HG], [1, P]], channel_multiplier=-1)
                    ins.then_inc(masked, 1)
                    if last and b in OUTPUT_MASKS:
                        divide_outputs(OUTPUT_MASKS.index(b))
                    if b == 4 and not last:
                        stage_values(n + 1, (r + 1) % N_RING)

            for p in range(2):
                reached(pool, v_used[p], PAIRS)
            stage_values(0, 0)
            group(0, 0, first=True)
            with pool.Fori(0, LOOPS) as it:
                for r in (1, 2, 3):
                    group(N_RING * it + r, r % N_RING)
            for n in range(N_RING * LOOPS + 1, N_GROUP):
                group(n, n % N_RING)

            inverse_deviations(2, 2 * (B - 1), 0, (B - 1) * KT)
            divide_outputs(B - 1)
            inverse_deviations(2, 2 * B, (B - 1) * KT, KT)

        @block.scalar
        def _(act):
            for one in start_at_one:
                act.sem_inc(one, 1)

            def copy_transposed(f, it, p):
                reached(act, tp_ready[f][p], it + 1)
                reached(act, v_ready[p] if f == 1 else gates_ready[f][p], it)
                nc.scalar.copy(xnt[p][:], work[p][:]).then_inc(xnt_ready[f][p], 1)
                if f != 1:
                    nc.scalar.copy(xnt_all[:, ds(it * 2 * CH + p * CH, CH)], work[p][:]).then_inc(xnt_saved[f][p], 1)

            def front(f):
                with act.Fori(0, PAIRS) as it:
                    for p in range(2):
                        copy_transposed(f, it, p)

            def split(n, it, p):
                reached(act, v_ready[p], it + 1)
                nc.scalar.copy(v_all[:, ds(it * G, G), p * TPC:(p + 1) * TPC, :],
                               v_ps[p][:].rearrange("p (k g f) -> p g k f", k=TPC, g=G)).then_inc(v_used[p], 1)
                reached(act, parts_written[p], 32 * it)
                for s in range(2):
                    act.wait_ge(rot_sum, 2 * n + s + 1)
                    nc.scalar.copy(parts[p][:, s, 0, :], rot_a[p][:, s, :]).then_inc(hi_ready, 1)

            def split_second(n, p):
                for s in range(2):
                    act.wait_ge(rest_ready[s], n + 1)
                    nc.scalar.copy(parts[p][:, s, 1, :], rest[:, s, :]).then_inc(mid_ready, 1)

            act.wait_ge(w_prod, 3)
            nc.scalar.copy(w_v[:], w_prod_ps["v"]).then_inc(w_ready, 1)
            front(0)
            for n in "qk":
                src = w_prod_ps[n].rearrange("p (g m r i d) -> p g m r i d", g=G, m=2, r=2, i=2)
                for r in range(2):
                    for g in range(G):
                        for m in range(2):
                            ins = nc.scalar.copy(w_qk[n][:, r, g, :, 2 * m:2 * m + 2],
                                                 src[:, g, m, r, :, :].rearrange("p i d -> p d i"))
            ins.then_inc(w_ready, 1)

            copy_transposed(1, 0, 0)
            copy_transposed(1, 0, 1)
            split(0, 0, 0)
            with act.Fori(0, PAIRS - 1) as it:
                copy_transposed(1, it + 1, 0)
                split(2 * it + 1, it, 1)
                split_second(2 * it, 0)
                copy_transposed(1, it + 1, 1)
                split(2 * it + 2, it + 1, 0)
                split_second(2 * it + 1, 1)
            split(2 * PAIRS - 1, PAIRS - 1, 1)
            split_second(2 * PAIRS - 2, 0)
            split_second(2 * PAIRS - 1, 1)

            def copy_outputs(n, r, turn, h):
                act.wait_ge(pv_done, N_BATCH * n + (N_BATCH - 2 if h == 0 else N_BATCH))
                if h == 0:
                    reached(act, y_written[r], 16 * HG * turn)
                nc.scalar.copy(y_sb[r][:, h * CH:(h + 1) * CH], y_ps[h][:]).then_inc(y_copied, 1)

            def group(n, r, turn, first=False):
                for s in range(N_SLOT):
                    act.wait_ge(st_ready, N_SLOT * n + s + 1)
                    if s % HG == 0:
                        atleast(act, pv_done, N_BATCH * n + s // HG + 1 - N_PBUF // HG)
                    nc.scalar.activation(prob[:, s % N_PBUF, :], st_ps[s % N_RING][:], ACT.Exp,
                                         scale=SCALE).then_inc(exp_done, 1)
                    for h in range(2):
                        if s == Y_COPY_SLOTS[h] and not first:
                            copy_outputs(n - 1, (r - 1) % N_RING, turn - (r == 0), h)

            group(0, 0, 0, first=True)
            with act.Fori(0, LOOPS) as it:
                for r in (1, 2, 3):
                    group(N_RING * it + r, r % N_RING, it + r // N_RING)
            for n in range(N_RING * LOOPS + 1, N_GROUP):
                group(n, n % N_RING, n // N_RING)
            for h in range(2):
                copy_outputs(N_GROUP - 1, (N_GROUP - 1) % N_RING, (N_GROUP - 1) // N_RING, h)

            front(2)

        @block.vector
        def _(v):
            chain = [0]

            def link(ins):
                chain[0] += 1
                ins.then_inc(dve, 1)
                v.wait_ge(dve, chain[0])

            def statistics(f, it, tiles):
                first = it * tiles
                for t in range(tiles):
                    ins = nc.vector.bn_stats(stats[:, t, :], x_sb[:, ds(first + t, 1), :].rearrange("p a c -> p (a c)"))
                ins.then_inc(stat_ready[f], 1)
                v.wait_ge(stat_ready[f], it + 1)
                apart(v, dve_passed)
                for t in range(tiles):
                    ins = nc.vector.bn_aggr(new_moments[:, t, :], stats[:, t, :])
                ins.then_inc(moments_ready[f], 1)
                v.wait_ge(moments_ready[f], it + 1)
                nc.vector.tensor_scalar(var_eps[:, ds(first, tiles)], new_moments[:, 0:tiles, 1], EPS, None,
                                        ALU.add).then_inc(var_ready[f], 1)
                nc.vector.tensor_copy(means[:, ds(first, tiles)], new_moments[:, 0:tiles, 0]).then_inc(means_ready[f], 1)

            def normalize(f, it, p):
                tile = it * 2 * TPC + p * TPC
                reached(v, tp_ready[f][p], it)
                for t in range(TPC):
                    ins = nc.vector.tensor_scalar(xn[p][:, t, :], x_sb[:, ds(tile + t, 1), :].rearrange("p a c -> p (a c)"),
                                                  means[:, ds(tile + t, 1)], rstd[:, ds(tile + t, 1)],
                                                  ALU.subtract, ALU.mult)
                ins.then_inc(xn_ready[f][p], 1)

            def ffn_front(f):
                with v.Fori(0, PAIRS) as it:
                    for p in range(2):
                        normalize(f, it, p)
                add_gate_biases(f)

            def add_gate_biases(f):
                for p in range(2):
                    reached(v, gates_ready[f][p], PAIRS)
                link(nc.vector.tensor_tensor(gates[:], gate_ps[:, 0:N_TILE * E].rearrange("p (t e) -> p t e", e=E),
                                             gb[:].rearrange("p (a e) -> p a e", a=1).broadcast_to([P, N_TILE, E]),
                                             ALU.add))

            def one_hot_of_best(values, hot):
                wide = best[:].broadcast_to([P, N_TILE, E])
                ranks = rank[:].rearrange("p (a e) -> p a e", a=1).broadcast_to([P, N_TILE, E])
                link(nc.vector.tensor_reduce(best[:], values, AX.X, ALU.max))
                link(nc.vector.tensor_tensor(hot, values, wide, ALU.is_equal))
                link(nc.vector.tensor_tensor(hot, hot, ranks, ALU.mult))
                link(nc.vector.tensor_reduce(best[:], hot, AX.X, ALU.max))
                link(nc.vector.tensor_tensor(hot, hot, wide, ALU.is_equal))

            def expert_weights(f):
                one_hot_of_best(gates[:], first[:])
                link(nc.vector.scalar_tensor_tensor(out=gate_tmp[:], in0=first[:], scalar=-BIG, in1=gates[:],
                                                    op0=ALU.mult, op1=ALU.add))
                one_hot_of_best(gate_tmp[:], second[:])
                link(nc.vector.tensor_tensor(first[:], first[:], second[:], ALU.add))
                nc.vector.tensor_reduce(counts[:], first[:].rearrange("p t e -> p e t"), AX.X,
                                        ALU.add).then_inc(cnt_ready[f], 1)
                v.wait_ge(cnt_sum[f], 1)
                link(nc.vector.tensor_scalar(weight[:], st_ps[0][:, 0:E], 0.5 / (N_TOK * TOP_K), None, ALU.mult))
                for some in (slice(0, 2), slice(2, E)):
                    width = some.stop - some.start
                    nc.vector.tensor_tensor(ews[:, some, :], ew[:, some, :],
                                            weight[:, some].rearrange("p (e a) -> p e a", a=1).broadcast_to(
                                                [P, width, C]), ALU.mult).then_inc(ews_ready[f], 1)
                link(nc.vector.tensor_tensor(neg_b[:], eb[:], weight[:], ALU.mult))
                link(nc.vector.tensor_reduce(b_sum[:], neg_b[:], AX.X, ALU.add))
                link(nc.vector.tensor_scalar(neg_b[:], neg_b[:], -1.0, None, ALU.mult))

            def experts(f):
                with v.Fori(0, PAIRS) as it:
                    for e in range(E):
                        for p in range(2):
                            i = 2 * (e % 2) + p
                            v.wait_ge(exp_ready[f][i], it * (E // 2) + e // 2 + 1)
                            if e == 0:
                                reached(v, back_ready[f][p], it)
                                nc.vector.tensor_scalar(acc[p][:], exp_ps[i][:], neg_b[:, 0:1], b_sum[:],
                                                        ALU.max, ALU.add).then_inc(exp_used[f][i], 1)
                            else:
                                reached(v, exp_used[f][2 * ((e - 1) % 2) + p], it * (E // 2) + (e - 1) // 2 + 1)
                                nc.vector.scalar_tensor_tensor(
                                    out=acc[p][:], in0=exp_ps[i][:], scalar=neg_b[:, e:e + 1], in1=acc[p][:],
                                    op0=ALU.max, op1=ALU.add).then_inc(exp_used[f][i], 1)
                    for p in range(2):
                        reached(v, back_ready[f][p], it + 1)
                        tiles = x_sb[:, ds(it * 2 * TPC + p * TPC, TPC), :]
                        nc.vector.tensor_tensor(tiles, tiles, work[p][:].rearrange("p (t c) -> p t c", c=C),
                                                ALU.add).then_inc(x_done[f][p], 1)
                    if f == 0:
                        reached(v, x_done[f][1], it + 1)
                        apart(v, dve_passed)
                        statistics(1, it, 2 * TPC)

            nc.vector.memset(pmax[:], -BIG)
            v.wait_ge(x_loaded, 16 * B)
            statistics(0, 0, N_TILE)
            v.wait_ge(w_loaded, 16 * 20)
            for n in "qk":
                even, odd = up[n][:, 0, :, DHE:DH:2], up[n][:, 0, :, DHE + 1:DH:2]
                nc.vector.tensor_scalar(up[n][:, 1, :, DHE:DH:2], odd, -1.0, None, ALU.mult).then_inc(rot_w, 1)
                nc.vector.tensor_copy(up[n][:, 1, :, DHE + 1:DH:2], even).then_inc(rot_w, 1)
            v.wait_ge(consts, 11)
            v.wait_ge(means_ready[0], 1)
            v.wait_ge(rstd_ready[0], 1)
            ffn_front(0)
            expert_weights(0)
            experts(0)

            def rotate(n, p):
                for s in range(2):
                    for r, (dst, table) in enumerate(((rot_a[p], cos_sb), (rot_b, sin_sb))):
                        i = 2 * s + r
                        v.wait_ge(qk_ready[i], n + 1)
                        if i == 0:
                            if not (isinstance(n, int) and n == 0):
                                reached(v, lo_ready, 2 * n - 2)
                        elif r == 1 and not (isinstance(n, int) and n == 0):
                            v.wait_ge(rot_sum, 2 * n + s - 1)
                        nc.vector.tensor_tensor(dst[:, s, :], qk_ps[i], table[:, p * CH:(p + 1) * CH],
                                                ALU.mult).then_inc(qk_used[i], 1)
                for s in range(2):
                    reached(v, qk_used[2 * s + 1], n + 1)
                    nc.vector.tensor_tensor(rot_a[p][:, s, :], rot_a[p][:, s, :], rot_b[:, s, :],
                                            ALU.add).then_inc(rot_sum, 1)

            def split(n, p):
                v.wait_ge(hi_ready, 2 * n + 1)
                reached(v, lo_ready, 2 * n)
                nc.vector.tensor_tensor(rest[:, 0, :], rot_a[p][:, 0, :], parts[p][:, 0, 0, :],
                                        ALU.subtract).then_inc(rest_ready[0], 1)

            v.wait_ge(means_ready[1], PAIRS)
            v.wait_ge(rstd_ready[1], PAIRS)
            normalize(1, 0, 0)
            normalize(1, 0, 1)
            normalize(1, 1, 0)
            rotate(0, 0)

            def two_chunks(it, last=False):
                normalize(1, it + 1, 1)
                rotate(2 * it + 1, 1)
                split(2 * it, 0)
                if not last:
                    normalize(1, it + 2, 0)
                rotate(2 * it + 2, 0)
                split(2 * it + 1, 1)

            with v.Fori(0, PAIRS - 2) as it:
                two_chunks(it)
            two_chunks(PAIRS - 2, last=True)
            rotate(2 * PAIRS - 1, 1)
            split(2 * PAIRS - 2, 0)
            split(2 * PAIRS - 1, 1)

            def maxima_unit(n, r, i):
                owner, j, pieces = UNITS[i]
                w = (N_UNIT * r + i) % N_RING
                v.wait_ge(unit_ready, units_done(n, i))
                if pieces is None:
                    rows = work[w][0:2 * KT, 0:P]
                    atleast(v, m_loaded, 4 * 16 * (n + owner))
                    nc.vector.tensor_copy(m_parts[j][:, 0, :], rows).then_inc(m_hi, 1)
                    v.wait_ge(m_hi, 2 * (n + owner) + j + 1)
                    nc.vector.tensor_tensor(m_parts[j][:, 1, :], rows, m_parts[j][:, 0, :],
                                            ALU.subtract).then_inc(unit_used, 1)
                    return
                qt, k0, tiles = pieces[0]
                if k0 == qt:
                    apart(v, dve_passed)
                    for c, (qt, _, _) in enumerate(pieces):
                        ins = nc.vector.tensor_tensor_reduce(junk[:, w, c, :], work[w][:, c * P:(c + 1) * P], causal[:],
                                                             1.0, -BIG, ALU.add, ALU.max, pmax[:, j, qt, 0:1])
                else:
                    step = pieces[1][0] - qt if len(pieces) > 1 else 1
                    c = reduced_column(pieces)
                    ins = nc.vector.tensor_reduce(pmax[:, j, qt:pieces[-1][0] + 1:step, c:c + 1],
                                                  work[w][:].rearrange("p (a t) -> p a t", t=tiles * P), AX.X, ALU.max)
                ins.then_inc(unit_used, 1)
                if i in HALF_ENDS:
                    h = j // 2
                    v.wait_ge(unit_used, units_done(n, i))
                    nc.vector.tensor_reduce(neg_max[:, h * 2 * KT:(h + 1) * 2 * KT],
                                            pmax[:, 2 * h:2 * h + 2, :, :].rearrange("p j k c -> p (j k) c"),
                                            AX.X, ALU.max, negate=True).then_inc(neg_max_ready, 1)

            def add_outputs(it, banks):
                for p in range(2):
                    reached(v, attn_ready[p], it + 1)
                    tiles = x_sb[:, ds(it * 2 * TPC + p * TPC, TPC), :]
                    nc.vector.tensor_tensor(tiles, tiles, banks[p][:].rearrange("p (t c) -> p t c", c=C),
                                            ALU.add).then_inc(attn_added[p], 1)
                    reached(v, attn_added[p], it + 1)
                    statistics(2, 2 * it + p, TPC)

            def group(n, r, first=False):
                for s in range(N_SLOT):
                    for d, i in units_beside(s):
                        if in_range(n + d, i):
                            maxima_unit(n + d, (r + d) % N_RING, i)
                    if s == (0 if isinstance(n, int) and n == N_GROUP - 1 else N_SLOT // 2) and not first:
                        invert(n - 1)
                if isinstance(n, int) and n == N_GROUP - 1:
                    for it in range(B - 1):
                        add_outputs(it, work)

            def invert(n):
                v.wait_ge(den_loaded, 16 * HG * (n + 1))
                atleast(v, rec_written, 16 * n)
                nc.vector.reciprocal(rec[:], den[:]).then_inc(rec_ready, 1)

            for k in range(N_UNIT + AHEAD):
                if in_range(k // N_UNIT, k % N_UNIT):
                    maxima_unit(k // N_UNIT, k // N_UNIT, k % N_UNIT)
            group(0, 0, first=True)
            with v.Fori(0, LOOPS) as it:
                for r in (1, 2, 3):
                    group(N_RING * it + r, r % N_RING)
            for n in range(N_RING * LOOPS + 1, N_GROUP):
                group(n, n % N_RING)

            invert(N_GROUP - 1)

            v.wait_ge(means_ready[2], 2 * (B - 1))
            v.wait_ge(rstd_ready[2], 1)
            with v.Fori(0, B - 1) as it:
                for p in range(2):
                    normalize(2, it, p)
            add_outputs(B - 1, y_ps)
            v.wait_ge(means_ready[2], 2 * B)
            v.wait_ge(rstd_ready[2], 2)
            for p in range(2):
                normalize(2, B - 1, p)
            add_gate_biases(2)
            expert_weights(2)
            experts(2)

        @block.tensor
        def _(pe):
            def transpose_chunk(f, it, p):
                pe.wait_ge(xn_ready[f][p], it + 1)
                reached(pe, xnt_ready[f][p], it)
                if f != 1:
                    reached(pe, xnt_saved[f][p], it)
                for t in range(TPC):
                    ins = nc.tensor.transpose(work[p][:, t * P:(t + 1) * P], xn[p][:, t, :], ident[:])
                ins.then_inc(tp_ready[f][p], 1)

            def gate_products(f, it, p):
                reached(pe, xnt_ready[f][p], it + 1)
                tile = it * 2 * TPC + p * TPC
                for t in range(TPC):
                    ins = nc.tensor.matmul(gate_ps[:, ds((tile + t) * E, E)], xnt[p][:, t * P:(t + 1) * P], gw[:],
                                           start=True, stop=True)
                ins.then_inc(gates_ready[f][p], 1)

            def ffn_front(f, start=0, end=PAIRS):
                transpose_chunk(f, start, 0)
                if end - start > 1:
                    with pe.Fori(start, end - 1) as it:
                        transpose_chunk(f, it, 1)
                        gate_products(f, it, 0)
                        transpose_chunk(f, it + 1, 0)
                        gate_products(f, it, 1)
                transpose_chunk(f, end - 1, 1)
                for p in range(2):
                    gate_products(f, end - 1, p)

            def experts(f):
                pe.wait_ge(cnt_ready[f], 1)
                nc.tensor.matmul(st_ps[0][:, 0:E], ones[:], counts[:], start=True, stop=True).then_inc(cnt_sum[f], 1)
                pe.wait_ge(ews_ready[f], 1)
                for p in range(2):
                    reached(pe, xnt_saved[f][p], PAIRS)
                with pe.Fori(0, PAIRS) as it:
                    for e in range(E):
                        if e == 2:
                            pe.wait_ge(ews_ready[f], 2)
                        for p in range(2):
                            i = 2 * (e % 2) + p
                            reached(pe, exp_used[f][i], it * (E // 2) + e // 2)
                            nc.tensor.matmul(exp_ps[i][:], ews[:, e, :], xnt_all[:, ds(it * 2 * CH + p * CH, CH)],
                                             start=True, stop=True).then_inc(exp_ready[f][i], 1)
                    for p in range(2):
                        reached(pe, exp_used[f][2 + p], it * (E // 2) + E // 2)
                        reached(pe, x_done[f][p], it)
                        for t in range(TPC):
                            ins = nc.tensor.transpose(work[p][:, t * P:(t + 1) * P], acc[p][:, t * P:(t + 1) * P],
                                                      ident[:])
                        ins.then_inc(back_ready[f][p], 1)

            pe.wait_ge(rot_w, 4)
            for n, ps in w_prod_ps.items():
                width = 2 * DH * (1 if n == "v" else 2)
                for m in range(H // 2):
                    rhs = up[n][:].rearrange("p r i d -> p (r i d)")[:, 0:width]
                    ins = nc.tensor.matmul(ps[:, m * width:(m + 1) * width], down[n][:, m, :], rhs,
                                           start=True, stop=True)
                ins.then_inc(w_prod, 1)

            pe.wait_ge(consts, 11)
            ffn_front(0)
            experts(0)
            pe.wait_ge(w_ready, 2)

            def products(n, it, p):
                reached(pe, xnt_ready[1][p], it + 1)
                for i in range(4):
                    reached(pe, qk_used[i], n)
                    nc.tensor.matmul(qk_ps[i], w_qk["qk"[i // 2]][:, i % 2, :, :, :].rearrange("p g d j -> p (g d j)"),
                                     xnt[p][:], start=True, stop=True).then_inc(qk_ready[i], 1)
                reached(pe, v_used[p], it)
                for t in range(TPC):
                    ins = nc.tensor.matmul(v_ps[p][:, t * P:(t + 1) * P], xnt[p][:, t * P:(t + 1) * P], w_v[:],
                                           start=True, stop=True)
                ins.then_inc(v_ready[p], 1)

            transpose_chunk(1, 0, 0)
            with pe.Fori(0, PAIRS - 1) as it:
                transpose_chunk(1, it, 1)
                products(2 * it, it, 0)
                transpose_chunk(1, it + 1, 0)
                products(2 * it + 1, it, 1)
            transpose_chunk(1, PAIRS - 1, 1)
            for p in range(2):
                products(2 * PAIRS - 2 + p, PAIRS - 1, p)

            def maxima_unit(n, r, turn, i):
                owner, j, pieces = UNITS[i]
                w = (N_UNIT * r + i) % N_RING
                if i == 0:
                    pe.wait_ge(stack_loaded[r], 16 * N_STACK_DMA * (turn + 1))
                atleast(pe, unit_used, bank_free(n, i))
                if pieces is None:
                    pe.wait_ge(neg_max_ready, 2 * (n + owner) + j + 1)
                    ins = nc.tensor.transpose(work[w][0:2 * KT, 0:P], neg_max[:, j * 2 * KT:(j + 1) * 2 * KT],
                                              ident[:])
                else:
                    col = 0
                    for qt, k0, tiles in pieces:
                        ins = nc.tensor.matmul(work[w][:, col:col + tiles * P],
                                               stack_q[r][:, j, qt * P:(qt + 1) * P],
                                               stack_k[r][:, j, k0 * P:(k0 + tiles) * P],
                                               start=True, stop=True)
                        col += tiles * P
                ins.then_inc(unit_ready, 1)

            def scores(n, r, s):
                atleast(pe, exp_done, N_SLOT * n + s + 1 - N_RING)
                j, col = s % HG, 0
                for kt, q, w in KINDS[s // HG]:
                    ins = nc.tensor.matmul(st_ps[s % N_RING][:, col:col + w], stack_k[r][:, j, kt * P:(kt + 1) * P],
                                           stack_q[r][:, j, q:q + w], start=True, stop=True)
                    col += w
                ins.then_inc(st_ready, 1)

            def values(n, r, b, i):
                if i == 0 and b in MASKED:
                    pe.wait_ge(masked, len(MASKED) * n + MASKED.index(b) + 1)
                elif i == 0:
                    pe.wait_ge(exp_done, N_SLOT * n + HG * (b + 1))
                if b == 0:
                    pe.wait_ge(v_st_ready, n + 1)
                if b < 2:
                    atleast(pe, y_copied, 2 * n - 1 + b)
                col = sum(w for _, _, w in KINDS[b][:i])
                kt, q, w = KINDS[b][i]
                for j in range(HG):
                    ins = nc.tensor.matmul(y_ps[q // CH][j * HROW:(j + 1) * HROW, q % CH:q % CH + w],
                                           v_st[r][:, kt, j, :], prob[:, (HG * b + j) % N_PBUF, col:col + w],
                                           start=(kt == 0), stop=False, skip_group_check=True)
                if i == len(KINDS[b]) - 1:
                    ins.then_inc(pv_done, 1)

            def output_products(it, p, banks):
                reached(pe, y_norm[p], it + 1)
                reached(pe, attn_added[p], it)
                for t in range(TPC):
                    ins = nc.tensor.matmul(banks[p][:, t * P:(t + 1) * P], y_t[p][:, t * P:(t + 1) * P], wc_sb[:],
                                           start=True, stop=True)
                ins.then_inc(attn_ready[p], 1)

            def group(n, r, turn, first=False):
                pe.wait_ge(m_loaded, 4 * 16 * n + 4 * 16)
                last = isinstance(n, int) and n == N_GROUP - 1
                for s in range(N_SLOT):
                    scores(n, r, s)
                    for it, slots in enumerate(OUTPUT_SLOTS if last else ()):
                        if s in slots:
                            output_products(it, slots.index(s), work)
                    if s == LAST_VALUES and not first:
                        values(n - 1, (r - 1) % N_RING, N_BATCH - 1, 0)
                    for d, i in units_beside(s):
                        if in_range(n + d, i):
                            maxima_unit(n + d, (r + d) % N_RING, turn + (r + d) // N_RING, i)
                    for b, i in values_at(s):
                        values(n, r, b, i)

            for i in range(4):
                reached(pe, qk_used[i], 2 * PAIRS)
            for p in range(2):
                reached(pe, v_used[p], PAIRS)
            for k in range(N_UNIT + AHEAD):
                if in_range(k // N_UNIT, k % N_UNIT):
                    maxima_unit(k // N_UNIT, k // N_UNIT, 0, k % N_UNIT)
            group(0, 0, 0, first=True)
            with pe.Fori(0, LOOPS) as it:
                for r in (1, 2, 3):
                    group(N_RING * it + r, r % N_RING, it + r // N_RING)
            for n in range(N_RING * LOOPS + 1, N_GROUP):
                group(n, n % N_RING, n // N_RING)
            values(N_GROUP - 1, (N_GROUP - 1) % N_RING, N_BATCH - 1, 0)

            ffn_front(2, 0, B - 1)
            for p in range(2):
                output_products(B - 1, p, y_ps)
            ffn_front(2, B - 1, B)
            experts(2)


def rotation_tables():
    inv_freq = np.float32(1.0) / np.float32(10000.0) ** (np.arange(0, DHE, 2, dtype=np.float32) / np.float32(DHE))
    freqs = np.arange(T, dtype=np.float32)[:, None] * inv_freq[None, :]
    emb = np.concatenate((freqs, freqs), axis=-1)
    dim = (np.arange(P) // HG) % DH
    cos, sin = np.ones((P, T), np.float32), np.zeros((P, T), np.float32)
    for d in range(DHE, DH):
        cos[dim == d] = np.cos(emb[:, d - DHE])
        sin[dim == d] = np.sin(emb[:, d - DHE])
    return cos, sin


def kernel(L0_attn_x, L0_attn_Wq_down, L0_attn_Wk_down, L0_attn_Wv_down, L0_attn_Wq_up_c, L0_attn_Wq_up_e,
           L0_attn_Wk_up_c, L0_attn_Wk_up_e, L0_attn_Wv_up, L0_attn_Wc, L0_ffn_gate_w, L0_ffn_gate_b,
           L0_ffn_expert_w, L0_ffn_expert_b):
    import concourse.bacc as bacc
    from concourse.bass_utils import run_bass_kernel_spmd

    def lay(a):
        return np.ascontiguousarray(a)

    def down_rows(w):
        return lay(np.asarray(w).T.reshape(H // 2, 2 * L, C).transpose(1, 0, 2))

    cos, sin = rotation_tables()
    arrays = {
        "x": lay(np.asarray(L0_attn_x).reshape(N_TOK, C)),
        "wq_t": down_rows(L0_attn_Wq_down), "wk_t": down_rows(L0_attn_Wk_down), "wv_t": down_rows(L0_attn_Wv_down),
        "q_c": lay(L0_attn_Wq_up_c), "q_e": lay(L0_attn_Wq_up_e),
        "k_c": lay(L0_attn_Wk_up_c), "k_e": lay(L0_attn_Wk_up_e),
        "v_up": lay(L0_attn_Wv_up), "wc": lay(L0_attn_Wc),
        "gate_wt": lay(np.asarray(L0_ffn_gate_w).T), "gate_b": lay(L0_ffn_gate_b),
        "exp_wt": lay(np.asarray(L0_ffn_expert_w).transpose(2, 0, 1)),
        "exp_bt": lay(np.asarray(L0_ffn_expert_b).T),
        "cos": cos, "sin": sin,
    }
    nc = bacc.Bacc("TRN2", target_bir_lowering=False, num_devices=1)
    ins = {n: nc.dram_tensor(n, a.shape, mybir.dt.from_np(a.dtype), kind="ExternalInput").ap()
           for n, a in arrays.items()}
    out = nc.dram_tensor("out", (N_TOK, C), F32, kind="ExternalOutput").ap()
    build(nc, **ins, out=out)
    result = run_bass_kernel_spmd(nc, [arrays], core_ids=[0])
    return result.results[0]["out"].reshape(B, T, C)
```
